# Optimizing a Trainium2 kernel written in Bass

```python
import numpy as np
import jax
import jax.numpy as jnp

def _softmax(x, axis=-1):
    return jax.nn.softmax(x, axis=axis)

def _gelu(x):
    return jax.nn.gelu(x, approximate=True)

def _silu(x):
    return jax.nn.silu(x)

def _sigmoid(x):
    return jax.nn.sigmoid(x)

def _layernorm(x, axis=-1, eps=1e-05):
    m = jnp.mean(x, axis=axis, keepdims=True)
    v = jnp.var(x, axis=axis, keepdims=True)
    return (x - m) / jnp.sqrt(v + eps)

def _scatter_add(tgt, idx, src, axis=0):
    return tgt.at[idx].add(src)

def _segment_sum(src, seg, n):
    return jax.ops.segment_sum(src, seg, n)
kernel_name = 'mk_macaron_d1_jaxref_r4_b288b8'

def setup_inputs(seed: int=0):
    np.random.seed(seed)
    _w = jnp.asarray

    def _L0_attn_setup():
        import jax, jax.numpy as jnp
        import numpy as np
        HIDDEN = 256
        HEADS = 16
        HEAD_DIM = HIDDEN // HEADS
        ROPE_BASE = 10000.0

        def _rope_cos_sin(seq_len, dim):
            inv_freq = 1.0 / ROPE_BASE ** (jnp.arange(0, dim, 2, dtype=jnp.float32) / dim)
            t = jnp.arange(seq_len, dtype=jnp.float32)
            freqs = jnp.einsum('i,j->ij', t, inv_freq)
            emb = jnp.concatenate([freqs, freqs], axis=-1)
            return (jnp.cos(emb), jnp.sin(emb))

        def _apply_rope(x, cos, sin):
            x1, x2 = (x[..., 0::2], x[..., 1::2])
            c = cos[..., :x1.shape[-1]]
            s = sin[..., :x1.shape[-1]]
            return jnp.concatenate([x1 * c - x2 * s, x1 * s + x2 * c], axis=-1)
        key = jax.random.key(seed)
        ks = jax.random.split(key, 9)
        B, S = (4, 512)
        lim = 1.0 / np.sqrt(HIDDEN)

        def lin(kw, kb):
            W = jax.random.uniform(kw, (HIDDEN, HIDDEN), jnp.float32, -lim, lim)
            b = jax.random.uniform(kb, (HIDDEN,), jnp.float32, -lim, lim)
            return (W, b)
        Wq, bq = lin(ks[0], ks[1])
        Wk, bk = lin(ks[2], ks[3])
        Wv, bv = lin(ks[4], ks[5])
        Wo, bo = lin(ks[6], ks[7])
        x = jax.random.normal(ks[8], (B, S, HIDDEN), jnp.float32)
        return {'x': x, 'Wq': Wq, 'bq': bq, 'Wk': Wk, 'bk': bk, 'Wv': Wv, 'bv': bv, 'Wo': Wo, 'bo': bo}
    _L0_attn_in = _L0_attn_setup()

    def _L0_ffn_setup():
        import jax, jax.numpy as jnp
        import numpy as np
        B, T, D, E, TOP_K = (4, 1024, 256, 8, 2)
        CAPACITY_FACTOR = 1.5
        key = jax.random.key(seed)
        k1, k2, k3 = jax.random.split(key, 3)
        x = jax.random.normal(k1, (B, T, D), dtype=jnp.float32)
        Wr = jax.random.normal(k2, (E, D), dtype=jnp.float32) * 0.02
        We = jax.random.normal(k3, (E, D, D), dtype=jnp.float32) * 0.02
        return {'x': x, 'Wr': Wr, 'We': We}
    _L0_ffn_in = _L0_ffn_setup()
    _d = {'L0_attn_x': _L0_attn_in['x'], 'L0_attn_Wq': _L0_attn_in['Wq'], 'L0_attn_bq': _L0_attn_in['bq'], 'L0_attn_Wk': _L0_attn_in['Wk'], 'L0_attn_bk': _L0_attn_in['bk'], 'L0_attn_Wv': _L0_attn_in['Wv'], 'L0_attn_bv': _L0_attn_in['bv'], 'L0_attn_Wo': _L0_attn_in['Wo'], 'L0_attn_bo': _L0_attn_in['bo'], 'L0_ffn_Wr': _L0_ffn_in['Wr'], 'L0_ffn_We': _L0_ffn_in['We']}
    _x0 = _d['L0_attn_x']
    _d['L0_attn_x'] = jax.random.normal(jax.random.fold_in(jax.random.key(seed), 1), (2, 4096, 256), dtype=_x0.dtype)
    del _x0
    return _d

def reference(L0_attn_x, L0_attn_Wq, L0_attn_bq, L0_attn_Wk, L0_attn_bk, L0_attn_Wv, L0_attn_bv, L0_attn_Wo, L0_attn_bo, L0_ffn_Wr, L0_ffn_We):

    def _L0_attn_ref(x, Wq, bq, Wk, bk, Wv, bv, Wo, bo):
        import jax, jax.numpy as jnp
        import numpy as np
        HIDDEN = 256
        HEADS = 16
        HEAD_DIM = HIDDEN // HEADS
        ROPE_BASE = 10000.0

        def _rope_cos_sin(seq_len, dim):
            inv_freq = 1.0 / ROPE_BASE ** (jnp.arange(0, dim, 2, dtype=jnp.float32) / dim)
            t = jnp.arange(seq_len, dtype=jnp.float32)
            freqs = jnp.einsum('i,j->ij', t, inv_freq)
            emb = jnp.concatenate([freqs, freqs], axis=-1)
            return (jnp.cos(emb), jnp.sin(emb))

        def _apply_rope(x, cos, sin):
            x1, x2 = (x[..., 0::2], x[..., 1::2])
            c = cos[..., :x1.shape[-1]]
            s = sin[..., :x1.shape[-1]]
            return jnp.concatenate([x1 * c - x2 * s, x1 * s + x2 * c], axis=-1)
        B, S, _ = x.shape
        scale = HEAD_DIM ** (-0.5)

        def proj(W, b):
            y = jnp.einsum('bsd,ed->bse', x, W) + b
            return y.reshape(B, S, HEADS, HEAD_DIM).transpose(0, 2, 1, 3)
        q = proj(Wq, bq)
        k = proj(Wk, bk)
        v = proj(Wv, bv)
        cos, sin = _rope_cos_sin(S, HEAD_DIM)
        cos = cos[None, None]
        sin = sin[None, None]
        q = _apply_rope(q, cos, sin) * scale
        k = _apply_rope(k, cos, sin)
        attn = jnp.einsum('bhsd,bhtd->bhst', q, k)
        attn = jax.nn.softmax(attn, axis=-1)
        out = jnp.einsum('bhst,bhtd->bhsd', attn, v)
        out = out.transpose(0, 2, 1, 3).reshape(B, S, HIDDEN)
        return jnp.einsum('bsd,ed->bse', out, Wo) + bo

    def _L0_ffn_ref(x, Wr, We):
        import jax, jax.numpy as jnp
        import numpy as np
        B, T, D, E, TOP_K = (4, 1024, 256, 8, 2)
        CAPACITY_FACTOR = 1.5
        Bb, Tt, Dd = x.shape
        Ee = Wr.shape[0]
        K = TOP_K
        C = int(Tt * K / Ee * CAPACITY_FACTOR) + 1
        logits = jnp.einsum('btd,ed->bte', x, Wr)
        top_vals, top_idx = jax.lax.top_k(logits, K)
        w = jax.nn.softmax(top_vals, axis=-1)
        flat_e = top_idx.reshape(Bb, Tt * K)
        oh = jax.nn.one_hot(flat_e, Ee, dtype=jnp.int32)
        pos_all = jnp.cumsum(oh, axis=1) - oh
        pos = jnp.take_along_axis(pos_all, flat_e[..., None], axis=-1)[..., 0]
        keep = pos < C
        b_idx = jnp.arange(Bb, dtype=jnp.int32)[:, None]
        dst = (b_idx * Ee + flat_e) * C + pos
        dst = jnp.where(keep, dst, Bb * Ee * C).reshape(-1)
        x_rep = jnp.repeat(x, K, axis=1).reshape(-1, Dd)
        buf = jnp.zeros((Bb * Ee * C, Dd), dtype=x.dtype).at[dst].add(x_rep, mode='drop')
        expert_in = buf.reshape(Bb, Ee, C, Dd)
        expert_out = jnp.einsum('becd,edf->becf', expert_in, We)
        gathered = jnp.take(expert_out.reshape(Bb * Ee * C, Dd), dst, axis=0, mode='fill', fill_value=0.0)
        gathered = gathered.reshape(Bb, Tt, K, Dd)
        out = jnp.einsum('btk,btkd->btd', w, gathered)
        return out
    x = L0_attn_x
    x = x + 0.5 * _L0_ffn_ref(_layernorm(x, axis=-1), L0_ffn_Wr, L0_ffn_We)
    x = x + _L0_attn_ref(_layernorm(x, axis=-1), L0_attn_Wq, L0_attn_bq, L0_attn_Wk, L0_attn_bk, L0_attn_Wv, L0_attn_bv, L0_attn_Wo, L0_attn_bo)
    x = x + 0.5 * _L0_ffn_ref(_layernorm(x, axis=-1), L0_ffn_Wr, L0_ffn_We)
    return x

_drawn_inputs = setup_inputs


def setup_inputs(seed=0):
    import zlib

    import numpy as np

    out = dict(_drawn_inputs(seed))
    spreads = {}
    factors = {'L0_attn_Wq': 8.0,
     'L0_attn_bq': 8.0,
     'L0_attn_Wk': 8.0,
     'L0_attn_bk': 8.0,
     'L0_attn_Wv': 6.153,
     'L0_attn_bv': 4.923,
     'L0_attn_bo': 3.107}
    for name, (base, spread) in spreads.items():
        noise = np.random.default_rng([zlib.crc32(name.encode()), seed]).standard_normal(out[name].shape)
        drawn = base * np.exp(spread * noise) if base else spread * noise
        out[name] = jnp.asarray(drawn.astype(out[name].dtype))
    for name, factor in factors.items():
        out[name] = (out[name] * factor).astype(out[name].dtype)
    return out
```

```python
import concourse.bass as bass
import numpy as np
from concourse import mybir
from contextlib import ExitStack

F32 = mybir.dt.float32
BF16 = mybir.dt.bfloat16
ALU = mybir.AluOpType
ACT = mybir.ActivationFunctionType
AX = mybir.AxisListType

P = 128
B, S, D = 2, 4096, 256
H, HD = 16, 16
E, TOPK = 8, 2
CAP = int(S * TOPK / E * 1.5) + 1
EPS = 1e-5
NC = D // P
NT = B * S // P
TG = 4
GT = TG * P
NG = NT // TG
GB = NG // B
SCALE = HD ** -0.5
DMA = 16


def hold(eng, sem, value, tick):
    eng.wait_ge(sem, value)
    eng.sem_inc(tick, 1)


def stream(sp, load, store, stores):
    for u in range(2):
        load(u, u)
    with sp.Fori(0, NG // 2 - 1) as it:
        for u in range(2):
            store(it * 2 + u, u)
            load(it * 2 + (u + 2), u)
    for u in range(2):
        store(NG - 2 + u, u)
    for sems, n in stores:
        for u in range(2):
            sp.wait_ge(sems[u], DMA * (n * NG // 2 + 1))


class Chain:

    def __init__(self, eng, sem, per_round, rounds_done):
        self.eng, self.sem, self.per_round, self.n = eng, sem, per_round, 0
        self.base = rounds_done * per_round if rounds_done is not None else 0

    def add(self, ins):
        self.n += 1
        ins.then_inc(self.sem, 1)

    def settle(self):
        self.eng.wait_ge(self.sem, self.base + self.n)

    def step(self, ins):
        self.add(ins)
        self.settle()

    def close(self):
        assert self.per_round is None or self.n == self.per_round, self.n


def norm_phase(nc, name, x, xnT, consts, Wr=None, logits=None):
    with ExitStack() as ctx:
        def sb(n, shape, dt=F32):
            return ctx.enter_context(nc.sbuf_tensor(f"{name}_{n}", shape, dt))

        def sem(n):
            return nc.alloc_semaphore(f"{name}_{n}")

        ident_in, = consts
        ident = sb("ident", [P, P])
        wr = sb("wr", [P, NC, E])
        xg = [sb(f"x{u}", [P, TG, D]) for u in range(2)]
        xn = [sb(f"xn{u}", [P, TG, D]) for u in range(2)]
        xt = [sb(f"xt{u}", [P, NC, GT]) for u in range(2)]
        stats = [sb(f"stats{u}", [P, TG, 6]) for u in range(2)]
        mv = [sb(f"mv{u}", [P, TG, 2]) for u in range(2)]
        ve = [sb(f"ve{u}", [P, TG]) for u in range(2)]
        sd = [sb(f"sd{u}", [P, TG]) for u in range(2)]
        r0 = [sb(f"r0{u}", [P, TG]) for u in range(2)]
        r1 = [sb(f"r1{u}", [P, TG]) for u in range(2)]
        rs = [sb(f"rs{u}", [P, TG]) for u in range(2)]
        pT = [ctx.enter_context(nc.psum_tensor(f"{name}_pT{k}", [P, GT], F32)) for k in range(2 * NC)]
        pL = [ctx.enter_context(nc.psum_tensor(f"{name}_pL{u}", [P, GT], F32)) for u in range(2)]

        s_const = sem("const")
        s_x = [sem(f"x{u}") for u in range(2)]
        s_st = [sem(f"st{u}") for u in range(2)]
        s_ch = sem("chain")
        s_ve = sem("ve")
        s_sd = sem("sd")
        s_xn = sem("xn")
        s_tr = sem("tr")
        s_xt = sem("xt")
        s_lg = sem("lg")
        s_lc = sem("lc")
        s_tick = sem("tick")
        AHEAD = 2

        with nc.Block() as block:
            @block.sync
            def _(sp):
                sp.dma_start(ident[:, :], ident_in).then_inc(s_const, DMA)
                if Wr is not None:
                    sp.dma_start(wr[:, :, :], Wr).then_inc(s_const, DMA)

                def load(g, u):
                    sp.wait_ge(s_xn, g + 1)
                    sp.dma_start(xg[u][:, :, :], x[bass.ds(g, 1), :, :, :].rearrange("g p i d -> p (g i) d"))\
                      .then_inc(s_x[u], DMA)

                def store(g, u):
                    sp.wait_ge(s_xt, g + (1 + AHEAD))
                    sp.dma_start(xnT[bass.ds(g, 1), :, :, :].rearrange("g p c t -> p (g c) t"),
                                 xt[u][:, :, :]).then_inc(s_st[u], DMA)

                stream(sp, load, store, [(s_st, 1)])

            @block.vector
            def _(ve_):
                ve_.sem_inc(s_xn, AHEAD)
                if Wr is not None:
                    ve_.sem_inc(s_lc, AHEAD)
                with ve_.Fori(0, NG // 2) as it:
                    ch = Chain(ve_, s_ch, 2 * (2 + 5), it)
                    for u in range(2):
                        ve_.wait_ge(s_x[u], it * DMA + DMA)
                        for i in range(TG):
                            last = ve_.bn_stats(stats[u][:, i, :], xg[u][:, i, :])
                        ch.add(last)
                        hold(ve_, s_ch, ch.base + ch.n, s_tick)
                        for i in range(TG):
                            last = ve_.bn_aggr(mv[u][:, i, :], stats[u][:, i, :])
                        ch.step(last)
                        ve_.tensor_scalar(ve[u][:, :], mv[u][:, :, 1], EPS, None, ALU.add).then_inc(s_ve, 1)
                    for u in range(2):
                        ve_.wait_ge(s_sd, it * 2 + (u + 1))
                        ch.step(ve_.reciprocal(r0[u][:, :], sd[u][:, :]))
                        ch.step(ve_.tensor_tensor(r1[u][:, :], r0[u][:, :], r0[u][:, :], ALU.mult))
                        ch.step(ve_.tensor_tensor(rs[u][:, :], r1[u][:, :], ve[u][:, :], ALU.mult))
                        ch.step(ve_.tensor_scalar(r1[u][:, :], rs[u][:, :], -0.5, 1.5, ALU.mult, ALU.add))
                        ch.step(ve_.tensor_tensor(rs[u][:, :], r0[u][:, :], r1[u][:, :], ALU.mult))
                        ve_.wait_ge(s_tr, it * 2 + (u + 1))
                        for i in range(TG):
                            last = ve_.tensor_scalar(xn[u][:, i, :], xg[u][:, i, :], mv[u][:, i, 0:1],
                                                     rs[u][:, i:i + 1], ALU.subtract, ALU.mult)
                        last.then_inc(s_xn, 1)
                    if Wr is not None:
                        for u in range(2):
                            ve_.wait_ge(s_lg, it * 2 + (u + 1))
                            ve_.tensor_copy(logits[:, bass.ds(it * (2 * TG * E) + u * TG * E, TG * E)],
                                            pL[u][:, 0:TG * E]).then_inc(s_lc, 1)
                    ch.close()

            @block.scalar
            def _(ac):
                ac.sem_inc(s_xt, AHEAD)
                for u in range(2):
                    ac.sem_inc(s_st[u], DMA)
                with ac.Fori(0, NG // 2) as it:
                    for u in range(2):
                        ac.wait_ge(s_ve, it * 2 + (u + 1))
                        ac.activation(sd[u][:, :], ve[u][:, :], ACT.Sqrt).then_inc(s_sd, 1)
                    for u in range(2):
                        ac.wait_ge(s_tr, it * 2 + (u + 1 + AHEAD))
                        ac.wait_ge(s_st[u], it * DMA + DMA)
                        if Wr is not None:
                            ac.wait_ge(s_lc, it * 2 + (u + 1))
                        for c in range(NC):
                            last = ac.activation(xt[u][:, c, :], pT[NC * u + c][:, :], ACT.Copy)
                        last.then_inc(s_xt, 1)

            @block.tensor
            def _(pe):
                pe.sem_inc(s_tr, AHEAD)
                pe.wait_ge(s_const, DMA * (2 if Wr is not None else 1))
                with pe.Fori(0, NG // 2) as it:
                    for u in range(2):
                        pe.wait_ge(s_xn, it * 2 + (u + 1 + AHEAD))
                        pe.wait_ge(s_xt, it * 2 + (u + 1))
                        for c in range(NC):
                            for i in range(TG):
                                last = pe.transpose(pT[NC * u + c][:, i * P:(i + 1) * P],
                                                    xn[u][:, i, c * P:(c + 1) * P], ident[:, :])
                        last.then_inc(s_tr, 1)
                    if Wr is not None:
                        for u in range(2):
                            pe.wait_ge(s_xt, it * 2 + (u + 1 + AHEAD))
                            for i in range(TG):
                                for c in range(NC):
                                    last = pe.matmul(pL[u][:, i * E:(i + 1) * E],
                                                     xt[u][:, c, i * P:(i + 1) * P], wr[:, c, :],
                                                     start=(c == 0), stop=(c == NC - 1))
                            last.then_inc(s_lg, 1)


def route_phase(nc, name, logits, weight, consts):
    before_in, order_in = consts
    with ExitStack() as ctx:
        def sb(n, shape, dt=F32):
            return ctx.enter_context(nc.sbuf_tensor(f"{name}_{n}", shape, dt))

        N = NT * E
        before32 = sb("before32", [P, P])
        before = sb("before", [P, P], BF16)
        ones = sb("ones", [P, P], BF16)
        ones32 = sb("ones32", [P, NT])
        order = sb("order", [P, E])
        t1, t2 = sb("t1", [P, NT, E]), sb("t2", [P, NT, E])
        sel = [sb(f"sel{k}", [P, NT, E]) for k in range(TOPK)]
        top = [sb(f"top{k}", [P, NT]) for k in range(TOPK)]
        rank = sb("rank", [P, NT])
        wk = [sb(f"wk{k}", [P, NT]) for k in range(TOPK)]
        gap, den = sb("gap", [P, NT]), sb("den", [P, NT])
        chosen = sb("chosen", [P, NT, E], BF16)
        count = sb("count", [P, NT, E])
        upto = sb("upto", [P, NT, E])
        p_in = ctx.enter_context(nc.psum_tensor(f"{name}_p_in", [P, N], F32))
        p_all = ctx.enter_context(nc.psum_tensor(f"{name}_p_all", [P, N], F32))
        s_c, s_ch, s_g, s_e, s_ma, s_mm = (nc.alloc_semaphore(f"{name}_{n}")
                                           for n in ("const", "chain", "gap", "exp", "mask", "sums"))
        L = logits[:, :].rearrange("p (t e) -> p t e", e=E)

        def over_e(ap):
            return ap.unsqueeze(2).to_broadcast([P, NT, E])

        with nc.Block() as block:
            @block.sync
            def _(sp):
                sp.dma_start(before32[:, :], before_in).then_inc(s_c, DMA)
                sp.dma_start(order[:, :], order_in).then_inc(s_c, DMA)

            @block.vector
            def _(ve):
                ch = Chain(ve, s_ch, None, None)
                ve.memset(ones32[:, :], 1.0)
                ch.step(ve.memset(ones[:, :], 1.0))
                ve.wait_ge(s_c, 2 * DMA)
                ch.step(ve.tensor_copy(before[:, :], before32[:, :]))
                left = L
                for k in range(TOPK):
                    ch.step(ve.tensor_reduce(out=top[k][:, :], in_=left, op=ALU.max, axis=AX.X))
                    ch.step(ve.tensor_tensor(t1[:, :, :], left, over_e(top[k][:, :]), ALU.is_ge))
                    ch.step(ve.tensor_tensor(t2[:, :, :], t1[:, :, :],
                                             order[:, :].unsqueeze(1).to_broadcast([P, NT, E]), ALU.mult))
                    ch.step(ve.tensor_reduce(out=rank[:, :], in_=t2[:, :, :], op=ALU.max, axis=AX.X))
                    ch.step(ve.tensor_tensor(sel[k][:, :, :], t2[:, :, :], over_e(rank[:, :]), ALU.is_equal))
                    if k == 0:
                        ch.step(ve.scalar_tensor_tensor(out=upto[:, :, :], in0=sel[0][:, :, :], scalar=-3e38,
                                                        in1=L, op0=ALU.mult, op1=ALU.add))
                        left = upto[:, :, :]
                ch.step(ve.tensor_tensor(chosen[:, :, :], sel[0][:, :, :], sel[1][:, :, :], ALU.add))
                ve.sem_inc(s_ma, 1)
                ve.tensor_tensor(gap[:, :], top[1][:, :], top[0][:, :], ALU.subtract).then_inc(s_g, 1)
                ve.wait_ge(s_e, 1)
                ch.step(ve.tensor_scalar(den[:, :], wk[1][:, :], 1.0, None, ALU.add))
                ch.step(ve.reciprocal(wk[0][:, :], den[:, :]))
                ch.step(ve.tensor_tensor(gap[:, :], wk[1][:, :], wk[0][:, :], ALU.mult))
                ch.step(ve.tensor_tensor(t1[:, :, :], sel[0][:, :, :], over_e(wk[0][:, :]), ALU.mult))
                ch.step(ve.tensor_tensor(t2[:, :, :], sel[1][:, :, :], over_e(gap[:, :]), ALU.mult))
                ch.step(ve.tensor_tensor(sel[0][:, :, :], t1[:, :, :], t2[:, :, :], ALU.add))
                ve.wait_ge(s_mm, 1)
                ch.step(ve.tensor_copy(count[:, :, :].rearrange("p t e -> p (t e)"), p_all[:, :]))
                for b in range(B):
                    for e in range(E):
                        ts = slice(b * NT // B, (b + 1) * NT // B)
                        ve_last = ve.tensor_tensor_scan(out=upto[:, ts, e], data0=ones32[:, ts],
                                                        data1=count[:, ts, e], initial=0.0,
                                                        op0=ALU.mult, op1=ALU.add)
                ch.step(ve_last)
                ch.step(ve.tensor_tensor(t1[:, :, :], upto[:, :, :], count[:, :, :], ALU.subtract))
                ch.step(ve.tensor_tensor(t2[:, :, :].rearrange("p t e -> p (t e)"),
                                         t1[:, :, :].rearrange("p t e -> p (t e)"), p_in[:, :], ALU.add))
                ch.step(ve.tensor_scalar(t1[:, :, :], t2[:, :, :], float(CAP), 0.5, ALU.is_lt, ALU.mult))
                ch.step(ve.tensor_tensor(weight[:, :, :], t1[:, :, :], sel[0][:, :, :], ALU.mult))

            @block.scalar
            def _(ac):
                ac.wait_ge(s_g, 1)
                ac.activation(wk[1][:, :], gap[:, :], ACT.Exp).then_inc(s_e, 1)

            @block.tensor
            def _(pe):
                pe.wait_ge(s_ma, 1)
                ch_flat = chosen[:, :, :].rearrange("p t e -> p (t e)")
                pe.matmul(p_in[:, :], before[:, :], ch_flat, start=True, stop=True)
                pe.matmul(p_all[:, :], ones[:, :], ch_flat, start=True, stop=True).then_inc(s_mm, 1)


def expert_phase(nc, name, x, xnT, We, weight, out):
    EP = 2
    with ExitStack() as ctx:
        def sb(n, shape, dt=F32):
            return ctx.enter_context(nc.sbuf_tensor(f"{name}_{n}", shape, dt))

        def sem(n):
            return nc.alloc_semaphore(f"{name}_{n}")

        we = sb("we", [P, NC, E, D])
        xt = [sb(f"xt{u}", [P, NC, GT]) for u in range(2)]
        xg = [sb(f"x{u}", [P, TG, D]) for u in range(2)]
        acc = [sb(f"acc{u}", [P, TG, D]) for u in range(2)]
        acb = [sb(f"acb{u}", [P, TG, D]) for u in range(2)]
        wg = [sb(f"wg{u}", [P, TG, E]) for u in range(2)]
        ps = [ctx.enter_context(nc.psum_tensor(f"{name}_ps{k}", [P, EP * D], F32)) for k in range(8)]
        s_we = sem("we")
        s_xt = [sem(f"xt{u}") for u in range(2)]
        s_x = [sem(f"x{u}") for u in range(2)]
        s_st = [sem(f"st{u}") for u in range(2)]
        s_mm = sem("mm")
        s_ac = sem("acc")
        NP = E // EP
        PAIRS = TG * NP
        STEPS = TG * E
        BANKS = len(ps)

        with nc.Block() as block:
            @block.sync
            def _(sp):
                sp.dma_start(we[:, :, :, :], We).then_inc(s_we, DMA)

                def load(g, u):
                    sp.wait_ge(s_ac, g * STEPS + STEPS)
                    sp.dma_start(xt[u][:, :, :], xnT[bass.ds(g, 1), :, :, :].rearrange("g p c t -> p (g c) t"))\
                      .then_inc(s_xt[u], DMA)
                    sp.dma_start(xg[u][:, :, :], x[bass.ds(g, 1), :, :, :].rearrange("g p i d -> p (g i) d"))\
                      .then_inc(s_x[u], DMA)

                def store(g, u):
                    sp.wait_ge(s_ac, g * STEPS + 3 * STEPS)
                    sp.dma_start(out[bass.ds(g, 1), :, :, :].rearrange("g p i d -> p (g i) d"),
                                 acc[u][:, :, :]).then_inc(s_st[u], DMA)

                stream(sp, load, store, [(s_st, 1)])

            @block.tensor
            def _(pe):
                pe.wait_ge(s_we, DMA)
                with pe.Fori(0, NG // 2) as it:
                    for u in range(2):
                        pe.wait_ge(s_xt[u], it * DMA + DMA)
                        for i in range(TG):
                            pe.wait_ge(s_ac, it * (2 * STEPS) + ((u + 2) * STEPS + (i - 1) * E))
                            for k in range(NP):
                                for c in range(NC):
                                    last = pe.matmul(ps[(i % 2) * NP + k][:, :],
                                                     xt[u][:, c, i * P:(i + 1) * P],
                                                     we[:, c, EP * k:EP * k + EP, :].rearrange("p e f -> p (e f)"),
                                                     start=(c == 0), stop=(c == NC - 1))
                                last.then_inc(s_mm, 1)

            @block.vector
            def _(ve):
                ve.sem_inc(s_ac, 2 * STEPS)
                for u in range(2):
                    ve.sem_inc(s_st[u], DMA)
                with ve.Fori(0, NG // 2) as it:
                    ve_base = it * (2 * STEPS)
                    for u in range(2):
                        ve.wait_ge(s_x[u], it * DMA + DMA)
                        ve.wait_ge(s_st[u], it * DMA + DMA)
                        for i in range(TG):
                            for e in range(E):
                                n = u * STEPS + i * E + e
                                if e % EP == 0:
                                    ve.wait_ge(s_mm, it * (2 * PAIRS) + (u * PAIRS + i * NP + e // EP + 1))
                                if e:
                                    ve.wait_ge(s_ac, ve_base + (2 * STEPS + n))
                                src = xg if e == 0 else (acb, acc)[(e - 1) % 2]
                                dst = (acb, acc)[e % 2]
                                ve.scalar_tensor_tensor(
                                    out=dst[u][:, i, :],
                                    in0=ps[(i % 2) * NP + e // EP][:, (e % EP) * D:(e % EP + 1) * D],
                                    scalar=weight[:, bass.ds(it * (2 * TG) + u * TG + i, 1), e],
                                    in1=src[u][:, i, :], op0=ALU.mult, op1=ALU.add).then_inc(s_ac, 1)


def qkv_phase(nc, name, xnT, wts, biases, tables, parts, v_out):
    wqk_in, wv_in = wts
    bqk_in, bv_in = biases
    cos_in, sin_in = tables
    with ExitStack() as ctx:
        def sb(n, shape, dt=F32):
            return ctx.enter_context(nc.sbuf_tensor(f"{name}_{n}", shape, dt))

        def sem(n):
            return nc.alloc_semaphore(f"{name}_{n}")

        wqk, wv = sb("wqk", [P, NC, 4, P]), sb("wv", [P, NC, D])
        bqk, bv, bs = sb("bqk", [P, 4]), sb("bv", [P, D]), sb("bs", [P, 4])
        xt = [sb(f"xt{u}", [P, NC, GT]) for u in range(2)]
        cs = [sb(f"cs{u}", [P, 2, GT]) for u in range(2)]
        ev, od = sb("even", [P, 2, GT]), sb("odd", [P, 2, GT])
        ec, es, oc, os_ = (sb(n, [P, 2, GT]) for n in ("ec", "es", "oc", "os"))
        rot = sb("rot", [P, 2, 2, GT])
        r1, r2 = sb("rest1", [P, 2, 2, GT]), sb("rest2", [P, 2, 2, GT])
        pt = [[sb(f"part{n}{u}", [P, 2, 2, GT], BF16) for n in range(3)] for u in range(2)]
        vt = [sb(f"v{u}", [P, H, TG, HD]) for u in range(2)]
        pqk = [ctx.enter_context(nc.psum_tensor(f"{name}_pqk{k}", [P, GT], F32)) for k in range(4)]
        pv = [ctx.enter_context(nc.psum_tensor(f"{name}_pv{k}", [P, 2 * D], F32)) for k in range(4)]

        s_c = sem("const")
        s_bs = sem("bs")
        s_xt = [sem(f"xt{u}") for u in range(2)]
        s_cs = [sem(f"cs{u}") for u in range(2)]
        s_st = [sem(f"st{u}") for u in range(2)]
        s_sv = [sem(f"sv{u}") for u in range(2)]
        s_qk = sem("qk")
        s_v = sem("v")
        s_ev = sem("evac")
        s_vc = sem("vcopy")
        s_ch = sem("chain")
        s_po = sem("pool")
        s_r = sem("rot")
        s_hi = sem("hi")
        s_r1 = sem("r1")
        s_mi = sem("mid")
        s_lo = sem("lo")
        s_tick = sem("tick")
        N_PARTS = 3

        with nc.Block() as block:
            @block.sync
            def _(sp):
                for dst, src in ((wqk[:, :, :, :], wqk_in), (wv[:, :, :], wv_in), (bqk[:, :], bqk_in),
                                 (bv[:, :], bv_in)):
                    sp.dma_start(dst, src).then_inc(s_c, DMA)

                def load(g, u):
                    sp.wait_ge(s_lo, g + 1)
                    sp.dma_start(xt[u][:, :, :], xnT[bass.ds(g, 1), :, :, :].rearrange("g p c t -> p (g c) t"))\
                      .then_inc(s_xt[u], DMA)
                    for k, tab in enumerate((cos_in, sin_in)):
                        sp.dma_start(cs[u][:, k:k + 1, :], tab[:, bass.ds(g, 1), :]).then_inc(s_cs[u], DMA)

                def store(g, u):
                    hold(sp, s_vc, g + 3, s_tick)
                    sp.dma_start(v_out[:, :, bass.ds(g, 1), :].rearrange("p h g n -> p h (g n)"),
                                 vt[u][:, :, :, :].rearrange("p h i d -> p h (i d)")).then_inc(s_sv[u], DMA)
                    hold(sp, s_lo, g + 3, s_tick)
                    for n in range(N_PARTS):
                        for half in range(2):
                            for w in range(2):
                                sp.dma_start(
                                    parts[w][n, half, :, bass.ds(g, 1), :].rearrange("p g t -> p (g t)"),
                                    pt[u][n][:, half, w, :]).then_inc(s_st[u], DMA)

                stream(sp, load, store, [(s_st, 4 * N_PARTS), (s_sv, 1)])

            @block.tensor
            def _(pe):
                pe.wait_ge(s_c, 4 * DMA)
                with pe.Fori(0, NG // 2) as it:
                    for u in range(2):
                        pe.wait_ge(s_xt[u], it * DMA + DMA)
                        pe.wait_ge(s_ev, it * 2 + (u + 1))
                        for m in range(4):
                            for c in range(NC):
                                last = pe.matmul(pqk[m][:, :], wqk[:, c, m, :], xt[u][:, c, :],
                                                 start=(c == 0), stop=(c == NC - 1))
                        last.then_inc(s_qk, 1)
                        pe.wait_ge(s_vc, it * 2 + (u + 1))
                        for i in range(TG):
                            for c in range(NC):
                                last = pe.matmul(pv[2 * u + i // 2][:, (i % 2) * D:(i % 2 + 1) * D],
                                                 xt[u][:, c, i * P:(i + 1) * P], wv[:, c, :],
                                                 start=(c == 0), stop=(c == NC - 1))
                        last.then_inc(s_v, 1)

            @block.scalar
            def _(ac):
                ac.sem_inc(s_ev, 1)
                ac.wait_ge(s_c, 4 * DMA)
                ac.activation(bs[:, 0:2], bqk[:, 0:2], ACT.Copy, scale=SCALE)
                ac.activation(bs[:, 2:4], bqk[:, 2:4], ACT.Copy).then_inc(s_bs, 1)
                ac.wait_ge(s_bs, 1)
                with ac.Fori(0, NG // 2) as it:
                    for u in range(2):
                        ac.wait_ge(s_qk, it * 2 + (u + 1))
                        ac.wait_ge(s_r, it * 2 + (u + 1))
                        for m in range(4):
                            dst = (ev, od)[m % 2]
                            last = ac.activation(dst[:, m // 2, :], pqk[m][:, :], ACT.Identity,
                                                 bias=bs[:, m:m + 1], scale=SCALE if m < 2 else 1.0)
                        last.then_inc(s_ev, 1)
                        ac.wait_ge(s_st[u], it * (3 * 4 * DMA) + DMA)
                        ac.wait_ge(s_r, it * 2 + (u + 2))
                        ac.activation(pt[u][0][:, :, :, :], rot[:, :, :, :], ACT.Copy).then_inc(s_hi, 1)
                        ac.wait_ge(s_r1, it * 2 + (u + 1))
                        ac.activation(pt[u][1][:, :, :, :], r1[:, :, :, :], ACT.Copy).then_inc(s_mi, 1)

            @block.vector
            def _(ve):
                ve.sem_inc(s_r, 1)
                ve.sem_inc(s_vc, 2)
                ve.sem_inc(s_lo, 2)
                for u in range(2):
                    ve.sem_inc(s_st[u], DMA)
                    ve.sem_inc(s_sv[u], DMA)
                ve.wait_ge(s_c, 4 * DMA)
                with ve.Fori(0, NG // 2) as it:
                    ch = Chain(ve, s_ch, 2, it)
                    for u in range(2):
                        cos = cs[u][:, 0:1, :].to_broadcast([P, 2, GT])
                        sin = cs[u][:, 1:2, :].to_broadcast([P, 2, GT])
                        ve.wait_ge(s_cs[u], it * (2 * DMA) + 2 * DMA)
                        ve.wait_ge(s_ev, it * 2 + (u + 2))
                        ve.tensor_tensor(ec[:, :, :], ev[:, :, :], cos, ALU.mult)
                        ch.step(ve.tensor_tensor(os_[:, :, :], od[:, :, :], sin, ALU.mult))
                        ve.tensor_tensor(rot[:, 0, :, :], ec[:, :, :], os_[:, :, :], ALU.subtract)
                        ve.wait_ge(s_po, it * 2 + (u + 1))
                        ve.tensor_tensor(rot[:, 1, :, :], es[:, :, :], oc[:, :, :], ALU.add).then_inc(s_r, 1)
                        ve.wait_ge(s_v, it * 2 + (u + 1))
                        ve.wait_ge(s_sv[u], it * DMA + DMA)
                        for i in range(TG):
                            last = ve.tensor_tensor(
                                vt[u][:, :, i, :],
                                pv[2 * u + i // 2][:, (i % 2) * D:(i % 2 + 1) * D].rearrange("p (h d) -> p h d", d=HD),
                                bv[:, :].rearrange("p (h d) -> p h d", d=HD), ALU.add)
                        last.then_inc(s_vc, 1)
                        ve.wait_ge(s_hi, it * 2 + (u + 1))
                        ve.tensor_tensor(r1[:, :, :, :], rot[:, :, :, :], pt[u][0][:, :, :, :],
                                         ALU.subtract).then_inc(s_r1, 1)
                        ve.wait_ge(s_mi, it * 2 + (u + 1))
                        ve.tensor_tensor(pt[u][2][:, :, :, :], r1[:, :, :, :], pt[u][1][:, :, :, :],
                                         ALU.subtract).then_inc(s_lo, 1)
                    ch.close()

            @block.gpsimd
            def _(gp):
                with gp.Fori(0, NG // 2) as it:
                    for u in range(2):
                        cos = cs[u][:, 0:1, :].to_broadcast([P, 2, GT])
                        sin = cs[u][:, 1:2, :].to_broadcast([P, 2, GT])
                        gp.wait_ge(s_cs[u], it * (2 * DMA) + 2 * DMA)
                        gp.wait_ge(s_ev, it * 2 + (u + 2))
                        gp.wait_ge(s_r, it * 2 + (u + 1))
                        gp.tensor_tensor(es[:, :, :], ev[:, :, :], sin, ALU.mult)
                        gp.tensor_tensor(oc[:, :, :], od[:, :, :], cos, ALU.mult).then_inc(s_po, 1)


def attend_phase(nc, name, parts, v_in, A, consts):
    q_parts, k_parts = parts
    fold_in, ident_in = consts
    NH = B * H
    QB = 512
    SB = S // QB
    KT = S // P
    TQ = QB // P
    KC = 2
    TERMS = [(0, 0), (0, 1), (0, 2), (1, 0), (1, 1), (2, 0)]
    ROWS = HD * len(TERMS)
    NB = 3
    NS = 2
    QUAD = 4
    LAG = 2
    NQ = KT // QUAD
    NP = QUAD * (LAG + 1)
    PAIRS = TQ * S // (QB * KC)
    W = 32
    CH = 5
    with ExitStack() as ctx:
        def sb(n, shape, dt=F32):
            return ctx.enter_context(nc.sbuf_tensor(f"{name}_{n}", shape, dt))

        def sem(n):
            return nc.alloc_semaphore(f"{name}_{n}")

        Q = [sb(f"q{p}", [P, S], BF16) for p in range(NB)]
        K = [sb(f"k{p}", [P, S], BF16) for p in range(NB)]
        vst = [sb(f"vst{p}", [P, KT, HD]) for p in range(NB)]
        V = [sb(f"v{p}", [P, KT, W]) for p in range(NB)]
        Ex = [sb(f"ex{j}", [P, QB]) for j in range(NP)]
        O = sb("o", [P, QB])
        fold = sb("fold", [P, HD + 1])
        ident32 = sb("ident32", [P, P])
        ident = sb("ident", [P, P], BF16)
        mx = sb("mx", [P, TQ, PAIRS // TQ])
        nm, rest, rest2 = sb("nm", [P, TQ]), sb("rest", [P, TQ]), sb("rest2", [P, TQ])
        m3 = sb("m3", [P, TQ, 3], BF16)
        rec = sb("rec", [P, TQ, 1])
        ps = [ctx.enter_context(nc.psum_tensor(f"{name}_s{k}", [P, QB], F32)) for k in range(NS)]
        pm = [ctx.enter_context(nc.psum_tensor(f"{name}_m{k}", [P, KC * QB], F32)) for k in range(2)]
        po = ctx.enter_context(nc.psum_tensor(f"{name}_po", [P, QB], F32))
        px = ctx.enter_context(nc.psum_tensor(f"{name}_px", [P, QB], F32))
        fin = px[:, 0:TQ * (HD + 1)].rearrange("p (i d) -> p i d", d=HD + 1)

        s_c = sem("const")
        s_cc = sem("constcopy")
        s_ld = [sem(f"load{p}") for p in range(NB)]
        s_lv = [sem(f"loadv{p}") for p in range(NB)]
        s_vh = sem("vh")
        s_one = sem("ones")
        s_s = sem("scores")
        s_e = sem("exp")
        s_pv = sem("pv")
        s_m = sem("mtile")
        s_mr = sem("mred")
        s_ch = sem("chain")
        s_m3 = sem("m3")
        s_mt = sem("mt")
        s_mq = sem("mq")
        s_o = sem("o")
        s_f = sem("fold")
        s_tick = sem("tick")
        s_a = sem("a")
        LOADS = 2 * len(TERMS)

        def rows(t):
            return slice(HD * t, HD * (t + 1))

        def load(sp, p, h):
            for t, (a, b) in enumerate(TERMS):
                for dst, src in ((Q[p][rows(t), :], q_parts[a]), (K[p][rows(t), :], k_parts[b])):
                    sp.dma_start(dst, src[:, bass.ds(h, 1), :].rearrange("r h s -> r (h s)"))\
                      .then_inc(s_ld[p], DMA)
            sp.dma_start(vst[p][:, :, :],
                         v_in[:, bass.ds(h, 1), :].rearrange("p h n -> p (h n)").rearrange("p (k d) -> p k d", d=HD))\
              .then_inc(s_lv[p], DMA)

        def heads(eng, step):
            full = (NH - 2) // NB
            assert full * NB == NH - 2
            with eng.Fori(0, full) as n:
                for r in range(NB):
                    step(r, n * NB + r, n, True, True)
            step(0, NH - 2, full, True, False)
            step(1, NH - 1, full, False, False)

        with nc.Block() as block:
            @block.sync
            def _(sp):
                sp.dma_start(fold[:, :], fold_in).then_inc(s_c, DMA)
                sp.dma_start(ident32[:, :], ident_in).then_inc(s_c, DMA)
                load(sp, 0, 0)
                load(sp, 1, 1)

                def step(r, h, n, more, loads):
                    if loads:
                        hold(sp, s_pv, h * (SB * NQ) + (LAG + 1), s_tick)
                        hold(sp, s_vh, h + 1, s_tick)
                        load(sp, (r + 2) % NB, h + 2)

                heads(sp, step)

            @block.gpsimd
            def _(gp):
                for p in range(NB):
                    gp.memset(V[p][:, :, :], 0.0)
                gp.memset(O[:, :], 1.0).then_inc(s_one, 1)
                gp.wait_ge(s_one, 1)
                for p in range(NB):
                    last = gp.memset(V[p][:, :, HD:HD + 1], 1.0)
                last.then_inc(s_one, 1)
                gp.wait_ge(s_one, 2)

                def fill(p, n):
                    hold(gp, s_lv[p], n * DMA + DMA, s_tick)
                    gp.tensor_copy(V[p][:, :, 0:HD], vst[p][:, :, :]).then_inc(s_vh, 1)

                fill(0, 0)

                def step(r, h, n, more, loads):
                    if more:
                        gp.wait_ge(s_pv, h * (SB * NQ) + (LAG + 1))
                        fill((r + 1) % NB, n + (r + 1) // NB)

                heads(gp, step)

            @block.tensor
            def _(pe):
                pe.sem_inc(s_pv, LAG + 1)
                pe.wait_ge(s_cc, 1)
                pe.wait_ge(s_one, 2)

                def max_tile(k, p, sb_, w16):
                    i, c = divmod(k, S // QB)
                    if c % KC == 0:
                        pair = k // KC
                        pe.wait_ge(s_mr, w16 + (pair + 1))
                    ins = pe.matmul(pm[(k // KC) % 2][:, (c % KC) * QB:(c % KC + 1) * QB],
                                    Q[p][0:ROWS, bass.ds(sb_ * QB + i * P, P)],
                                    K[p][0:ROWS, c * QB:(c + 1) * QB], start=True, stop=True)
                    if c % KC == KC - 1:
                        ins.then_inc(s_m, 1)

                def rows_of_max(w):
                    pe.wait_ge(s_m3, w + 1)
                    for i in range(TQ):
                        last = pe.matmul(px[ROWS:ROWS + 3, i * P:(i + 1) * P], m3[:, i, :], ident[:, :],
                                         start=True, stop=True)
                    last.then_inc(s_mt, 1)

                def unit(main, find, p, sb_, u):
                    pn = (p + 1) % NB if main else p
                    if main:
                        w = u + SB
                        pe.wait_ge(s_mq, u + 2)
                    else:
                        w = u
                        pe.wait_ge(s_mq, w + 1)
                    w16 = w * PAIRS
                    e32 = u * KT
                    tiles = iter(range(TQ * S // QB))
                    for s in range(NQ + LAG):
                        if main and s < NQ:
                            for k in range(QUAD):
                                j = s * QUAD + k
                                pe.wait_ge(s_e, e32 + (j + 1))
                                pe.matmul(ps[j % NS][:, :], K[p][0:ROWS + 3, j * P:(j + 1) * P],
                                          Q[p][0:ROWS + 3, bass.ds(sb_ * QB, QB)],
                                          start=True, stop=True).then_inc(s_s, 1)
                                if find:
                                    max_tile(next(tiles), pn, sb_, w16)
                        if main and s == 1:
                            pe.wait_ge(s_o, u + 1)
                            if find:
                                pe.wait_ge(s_mq, w + 1)
                            else:
                                pe.wait_ge(s_mq, NH * SB + 1)
                                pe.wait_ge(s_a, u)
                            for i in range(TQ):
                                last = pe.matmul(fin[:, i, :], O[:, i * P:(i + 1) * P], fold[:, :],
                                                 start=True, stop=True)
                            last.then_inc(s_f, 1)
                        if main and s >= LAG:
                            q = s - LAG
                            if q == 0:
                                pe.wait_ge(s_o, u + 1)
                            pe.wait_ge(s_e, e32 + (QUAD * (q + 1) + NS))
                            for g in range(QUAD):
                                j = QUAD * q + g
                                last = pe.matmul(po[W * g:W * (g + 1), :], V[p][:, j, :],
                                                 Ex[j % NP][:, :], start=(q == 0), stop=(q == NQ - 1))
                            last.then_inc(s_pv, 1)
                    if find:
                        for k in tiles:
                            max_tile(k, pn, sb_, w16)
                        if main:
                            pe.wait_ge(s_a, u + 1)
                        rows_of_max(w)

                pe.wait_ge(s_ld[0], LOADS * DMA)
                with pe.Fori(0, SB) as sb_:
                    unit(False, True, 0, sb_, sb_)

                def step(r, h, n, more, loads):
                    hold(pe, s_vh, h + 1, s_tick)
                    if more:
                        hold(pe, s_ld[(r + 1) % NB], (n + (r + 1) // NB) * (LOADS * DMA) + LOADS * DMA, s_tick)
                    with pe.Fori(0, SB) as sb_:
                        unit(True, more, r, sb_, h * SB + sb_)

                heads(pe, step)
                pe.wait_ge(s_o, NH * SB + 1)
                pe.wait_ge(s_a, NH * SB)
                for i in range(TQ):
                    last = pe.matmul(fin[:, i, :], O[:, i * P:(i + 1) * P], fold[:, :], start=True, stop=True)
                last.then_inc(s_f, 1)

            @block.scalar
            def _(ac):
                ac.sem_inc(s_e, NS)
                ac.wait_ge(s_one, 1)
                ac.sem_inc(s_o, 1)

                def step(r, h, n, more, loads):
                    with ac.Fori(0, SB) as sb_:
                        u = h * SB + sb_
                        t32 = u * KT
                        q8 = u * NQ
                        for j in range(KT):
                            if j % QUAD == 0:
                                ac.wait_ge(s_pv, q8 + (j // QUAD + 1))
                            ac.wait_ge(s_s, t32 + (j + 1))
                            ac.activation(Ex[j % NP][:, :], ps[j % NS][:, :], ACT.Exp).then_inc(s_e, 1)
                        ac.wait_ge(s_pv, q8 + (NQ + LAG + 1))
                        ac.wait_ge(s_f, u + 1)
                        ac.activation(O[:, :], po[:, :], ACT.Copy).then_inc(s_o, 1)

                heads(ac, step)

            @block.vector
            def _(ve):
                ve.sem_inc(s_mr, 2)
                ve.sem_inc(s_mq, 1)
                ve.wait_ge(s_c, 2 * DMA)
                for p in range(NB):
                    ve.memset(K[p][ROWS:ROWS + 3, :], 1.0)
                ve.tensor_copy(ident[:, :], ident32[:, :]).then_inc(s_cc, 1)

                def find_max(k, w16):
                    ve.wait_ge(s_m, w16 + (k + 1))
                    return ve.tensor_reduce(out=mx[:, k // (PAIRS // TQ), k % (PAIRS // TQ):k % (PAIRS // TQ) + 1],
                                            in_=pm[k % 2][:, :], op=ALU.max, axis=AX.X).then_inc(s_mr, 1)

                def split_max(p, sb_, w):
                    ch = Chain(ve, s_ch, CH, w)
                    ve.wait_ge(s_mr, w * PAIRS + (PAIRS + 2))
                    ch.step(ve.tensor_reduce(out=nm[:, :], in_=mx[:, :, :], op=ALU.max, axis=AX.X, negate=True))
                    ch.step(ve.tensor_copy(m3[:, :, 0], nm[:, :]))
                    ch.step(ve.tensor_tensor(rest[:, :], nm[:, :], m3[:, :, 0], ALU.subtract))
                    ch.step(ve.tensor_copy(m3[:, :, 1], rest[:, :]))
                    ch.step(ve.tensor_tensor(rest2[:, :], rest[:, :], m3[:, :, 1], ALU.subtract))
                    ve.tensor_copy(m3[:, :, 2], rest2[:, :]).then_inc(s_m3, 1)
                    ch.close()
                    ve.wait_ge(s_mt, w + 1)
                    ve.tensor_copy(Q[p][ROWS:ROWS + 3, bass.ds(sb_ * QB, QB)],
                                   px[ROWS:ROWS + 3, :]).then_inc(s_mq, 1)

                def normalise(u):
                    ve.wait_ge(s_f, u + 1)
                    ve.reciprocal(rec[:, :, :], fin[:, :, HD:HD + 1]).then_inc(s_rc, 1)
                    ve.wait_ge(s_rc, u + 1)
                    ve.tensor_tensor(A[:, bass.ds(u, 1), :, :].rearrange("p u i d -> p (u i) d"),
                                     fin[:, :, 0:HD], rec[:, :, :].to_broadcast([P, TQ, HD]),
                                     ALU.mult).then_inc(s_a, 1)

                s_rc = nc.alloc_semaphore(f"{name}_rc")
                with ve.Fori(0, SB) as sb_:
                    w16 = sb_ * PAIRS
                    for k in range(PAIRS):
                        find_max(k, w16)
                    split_max(0, sb_, sb_)

                def step(r, h, n, more, loads):
                    with ve.Fori(0, SB) as sb_:
                        u = h * SB + sb_
                        w = u + SB
                        w16 = w * PAIRS
                        AT = 5
                        if more:
                            for k in range(AT):
                                find_max(k, w16)
                        normalise(u)
                        if more:
                            for k in range(AT, PAIRS):
                                find_max(k, w16)
                            split_max((r + 1) % NB, sb_, w)

                heads(ve, step)
                normalise(NH * SB)
                ve.wait_ge(s_a, NH * SB + 1)


def out_phase(nc, name, x, A, Wo, bo, consts, out):
    ident_in, = consts
    with ExitStack() as ctx:
        def sb(n, shape, dt=F32):
            return ctx.enter_context(nc.sbuf_tensor(f"{name}_{n}", shape, dt))

        def sem(n):
            return nc.alloc_semaphore(f"{name}_{n}")

        ident = sb("ident", [P, P])
        wo = sb("wo", [P, NC, D])
        bo_sb = sb("bo", [P, D])
        at = [sb(f"at{u}", [P, TG, D]) for u in range(2)]
        aT = [sb(f"aT{u}", [P, NC, GT]) for u in range(2)]
        xg = [sb(f"x{u}", [P, TG, D]) for u in range(2)]
        xb = [sb(f"xb{u}", [P, TG, D]) for u in range(2)]
        y = [sb(f"y{u}", [P, TG, D]) for u in range(2)]
        pT = [ctx.enter_context(nc.psum_tensor(f"{name}_pT{k}", [P, GT], F32)) for k in range(2 * NC)]
        py = [ctx.enter_context(nc.psum_tensor(f"{name}_py{k}", [P, 2 * D], F32)) for k in range(4)]
        s_c = sem("const")
        s_x = [sem(f"x{u}") for u in range(2)]
        s_st = [sem(f"st{u}") for u in range(2)]
        s_at = sem("at")
        s_tr = sem("tr")
        s_aT = sem("aT")
        s_y = sem("y")
        s_xb = sem("xb")
        s_o = sem("out")

        with nc.Block() as block:
            @block.sync
            def _(sp):
                for dst, src in ((ident[:, :], ident_in), (wo[:, :, :], Wo), (bo_sb[:, :], bo)):
                    sp.dma_start(dst, src).then_inc(s_c, DMA)

                def load(g, u):
                    sp.wait_ge(s_xb, g + 1)
                    sp.dma_start(xg[u][:, :, :], x[bass.ds(g, 1), :, :, :].rearrange("g p i d -> p (g i) d"))\
                      .then_inc(s_x[u], DMA)

                def store(g, u):
                    sp.wait_ge(s_o, g + 3)
                    sp.dma_start(out[bass.ds(g, 1), :, :, :].rearrange("g p i d -> p (g i) d"),
                                 y[u][:, :, :]).then_inc(s_st[u], DMA)

                stream(sp, load, store, [(s_st, 1)])

            @block.scalar
            def _(ac):
                ac.sem_inc(s_aT, 2)
                for b in range(B):
                    heads = A[:, 1:1 + H * B * GB, :, :].rearrange("p (h b s) i d -> p h b s i d", b=B, s=GB)
                    with ac.Fori(0, GB // 2) as it:
                        for u in range(2):
                            n = it * 2 + (b * GB + u)
                            ac.wait_ge(s_tr, n + 1)
                            for i in range(TG):
                                last = ac.activation(
                                    at[u][:, i, :].rearrange("p (h d) -> p h d", d=HD),
                                    heads[:, :, b, bass.ds(it * 2 + u, 1), i, :].rearrange("p h s d -> p h (s d)"),
                                    ACT.Copy)
                            last.then_inc(s_at, 1)
                        for u in range(2):
                            n = it * 2 + (b * GB + u)
                            ac.wait_ge(s_tr, n + 3)
                            ac.wait_ge(s_o, n + 1)
                            for c in range(NC):
                                last = ac.activation(aT[u][:, c, :], pT[NC * u + c][:, :], ACT.Copy)
                            last.then_inc(s_aT, 1)

            @block.tensor
            def _(pe):
                pe.sem_inc(s_tr, 2)
                pe.wait_ge(s_c, 3 * DMA)
                with pe.Fori(0, NG // 2) as it:
                    for u in range(2):
                        pe.wait_ge(s_at, it * 2 + (u + 1))
                        pe.wait_ge(s_aT, it * 2 + (u + 1))
                        for c in range(NC):
                            for i in range(TG):
                                last = pe.transpose(pT[NC * u + c][:, i * P:(i + 1) * P],
                                                    at[u][:, i, c * P:(c + 1) * P], ident[:, :])
                        last.then_inc(s_tr, 1)
                    for u in range(2):
                        pe.wait_ge(s_aT, it * 2 + (u + 3))
                        pe.wait_ge(s_o, it * 2 + (u + 1))
                        for i in range(TG):
                            for c in range(NC):
                                last = pe.matmul(py[2 * u + i // 2][:, (i % 2) * D:(i % 2 + 1) * D],
                                                 aT[u][:, c, i * P:(i + 1) * P], wo[:, c, :],
                                                 start=(c == 0), stop=(c == NC - 1))
                        last.then_inc(s_y, 1)

            @block.vector
            def _(ve):
                ve.sem_inc(s_xb, 2)
                ve.sem_inc(s_o, 2)
                for u in range(2):
                    ve.sem_inc(s_st[u], DMA)
                ve.wait_ge(s_c, 3 * DMA)
                with ve.Fori(0, NG // 2) as it:
                    for u in range(2):
                        ve.wait_ge(s_x[u], it * DMA + DMA)
                        for i in range(TG):
                            last = ve.tensor_tensor(xb[u][:, i, :], xg[u][:, i, :], bo_sb[:, :], ALU.add)
                        last.then_inc(s_xb, 1)
                    for u in range(2):
                        ve.wait_ge(s_y, it * 2 + (u + 1))
                        ve.wait_ge(s_xb, it * 2 + (u + 3))
                        ve.wait_ge(s_st[u], it * DMA + DMA)
                        for i in range(TG // 2):
                            last = ve.tensor_tensor(
                                y[u][:, 2 * i:2 * i + 2, :].rearrange("p i d -> p (i d)"), py[2 * u + i][:, :],
                                xb[u][:, 2 * i:2 * i + 2, :].rearrange("p i d -> p (i d)"), ALU.add)
                        last.then_inc(s_o, 1)


def program(nc, x, w, c, out):
    def grouped(ap):
        return ap.rearrange("(g i p) d -> g p i d", i=TG, p=P)

    def dram(n, shape, dt=F32):
        return nc.dram_tensor(n, shape, dt, kind="Internal").ap()

    x1 = dram("after_ffn1", (NG, P, TG, D))
    x2 = dram("after_attention", (NG, P, TG, D))
    xnT = dram("normalised", (NG, P, NC, GT))
    qk = [dram(f"{n}_parts", (3, 2, P, NG, GT), BF16) for n in "qk"]
    vd = dram("v_by_head", (P, H, NG, TG * HD))

    with ExitStack() as ctx:
        A = ctx.enter_context(nc.sbuf_tensor("attended", [P, 1 + B * H * GB, TG, HD], F32))
        logits = A[:, 0:NT * E // (TG * HD), :, :].rearrange("p u i d -> p (u i d)")
        weight = A[:, 64:64 + NT * E // (TG * HD), :, :].rearrange("p u i d -> p (u i d)")\
            .rearrange("p (t e) -> p t e", e=E)

        def moe(name, src, dst):
            norm_phase(nc, name + "n", src, xnT, (c["ident"],), w["Wr"], logits)
            route_phase(nc, name + "r", logits, weight, (c["before"], c["order"]))
            expert_phase(nc, name + "e", src, xnT, w["We"], weight, dst)

        moe("f1", grouped(x), x1)
        norm_phase(nc, "an", x1, xnT, (c["ident"],))
        qkv_phase(nc, "ap", xnT, (w["Wqk"], w["Wv"]), (w["bqk"], w["bv"]), (c["cos"], c["sin"]), qk, vd)
        attend_phase(nc, "at",
                     [[t[k].rearrange("f (j h) (b g) t -> (f j) (h b) (g t)", h=H, b=B) for k in range(3)] for t in qk],
                     vd.rearrange("p h (b g) n -> p (h b) (g n)", b=B), A, (c["fold"], c["ident"]))
        out_phase(nc, "ao", x1, A, w["Wo"], w["bo"], (c["ident"],), x2)
        moe("f2", x2, grouped(out))


def shape_constants():
    inv_freq = (np.float32(1.0) / np.float32(10000.0) ** (np.arange(0, HD, 2, dtype=np.float32) / np.float32(HD)))
    angle = np.arange(S, dtype=np.float32)[:, None] * inv_freq.astype(np.float32)[None, :]
    rows = np.repeat(np.arange(HD // 2), H)

    def table(f):
        t = f(angle).astype(np.float32)[:, rows].T.reshape(P, GB, GT)
        return np.ascontiguousarray(np.concatenate([t] * B, axis=1))

    fold = np.zeros((P, HD + 1), np.float32)
    for g in range(4):
        fold[32 * g:32 * g + HD + 1] = np.eye(HD + 1, dtype=np.float32)
    return {
        "ident": np.eye(P, dtype=np.float32),
        "before": np.triu(np.ones((P, P), np.float32), 1),
        "order": np.tile(np.arange(E, 0, -1, dtype=np.float32), (P, 1)),
        "fold": fold,
        "cos": table(np.cos),
        "sin": table(np.sin),
    }


def kernel(L0_attn_x, L0_attn_Wq, L0_attn_bq, L0_attn_Wk, L0_attn_bk, L0_attn_Wv, L0_attn_bv,
           L0_attn_Wo, L0_attn_bo, L0_ffn_Wr, L0_ffn_We):
    import concourse.bacc as bacc
    from concourse.bass_utils import run_bass_kernel_spmd

    def by_feature(a):
        return a.T.reshape(NC, P, -1).transpose(1, 0, 2)

    def halves(W):
        return [W.reshape(H, HD // 2, 2, -1)[:, :, k, :].transpose(1, 0, 2).reshape(P, -1) for k in range(2)]

    X = {n: np.asarray(a) for n, a in dict(
        x=L0_attn_x, Wq=L0_attn_Wq, bq=L0_attn_bq, Wk=L0_attn_Wk, bk=L0_attn_bk, Wv=L0_attn_Wv,
        bv=L0_attn_bv, Wo=L0_attn_Wo, bo=L0_attn_bo, Wr=L0_ffn_Wr, We=L0_ffn_We).items()}
    arrays = {
        "x": X["x"].reshape(B * S, D),
        "Wqk": np.stack([by_feature(m) for m in halves(X["Wq"]) + halves(X["Wk"])], axis=2),
        "bqk": np.concatenate(halves(X["bq"].reshape(D, 1)) + halves(X["bk"].reshape(D, 1)), axis=1),
        "Wv": by_feature(X["Wv"]),
        "bv": np.tile(X["bv"], (P, 1)),
        "Wo": by_feature(X["Wo"]),
        "bo": np.tile(X["bo"], (P, 1)),
        "Wr": by_feature(X["Wr"]),
        "We": X["We"].reshape(E, NC, P, D).transpose(2, 1, 0, 3),
    }
    consts = shape_constants()
    nc = bacc.Bacc("TRN2", target_bir_lowering=False, num_devices=1)
    given, aps = {}, {}
    for n, a in {**arrays, **{"c_" + k: v for k, v in consts.items()}}.items():
        given[f"in_{n}"] = np.ascontiguousarray(a)
        aps[n] = nc.dram_tensor(f"in_{n}", a.shape, F32, kind="ExternalInput").ap()
    out = nc.dram_tensor("out", (B * S, D), F32, kind="ExternalOutput").ap()
    program(nc, aps["x"], aps, {k: aps["c_" + k] for k in consts}, out)
    r = run_bass_kernel_spmd(nc, [given], core_ids=[0])
    return r.results[0]["out"].reshape(B, S, D)
```

```python
import concourse.bass as bass
import numpy as np
from concourse import mybir
from contextlib import ExitStack

F32 = mybir.dt.float32
BF16 = mybir.dt.bfloat16
ALU = mybir.AluOpType
ACT = mybir.ActivationFunctionType
AX = mybir.AxisListType

P = 128
B, S, D = 2, 4096, 256
H, HD = 16, 16
E, TOPK = 8, 2
CAP = int(S * TOPK / E * 1.5) + 1
EPS = 1e-5
NC = D // P
NT = B * S // P
TG = 4
GT = TG * P
NG = NT // TG
GB = NG // B
SCALE = HD ** -0.5
DMA = 16


def hold(eng, sem, value, tick):
    eng.wait_ge(sem, value)
    eng.sem_inc(tick, 1)


def stream(sp, load, store, stores):
    for u in range(2):
        load(u, u)
    with sp.Fori(0, NG // 2 - 1) as it:
        for u in range(2):
            store(it * 2 + u, u)
            load(it * 2 + (u + 2), u)
    for u in range(2):
        store(NG - 2 + u, u)
    for sems, n in stores:
        for u in range(2):
            sp.wait_ge(sems[u], DMA * (n * NG // 2 + 1))


class Chain:

    def __init__(self, eng, sem, per_round, rounds_done):
        self.eng, self.sem, self.per_round, self.n = eng, sem, per_round, 0
        self.base = rounds_done * per_round if rounds_done is not None else 0

    def add(self, ins):
        self.n += 1
        ins.then_inc(self.sem, 1)

    def settle(self):
        self.eng.wait_ge(self.sem, self.base + self.n)

    def step(self, ins):
        self.add(ins)
        self.settle()

    def close(self):
        assert self.per_round is None or self.n == self.per_round, self.n


def norm_phase(nc, name, x, xnT, consts, Wr=None, logits=None):
    with ExitStack() as ctx:
        def sb(n, shape, dt=F32):
            return ctx.enter_context(nc.sbuf_tensor(f"{name}_{n}", shape, dt))

        def sem(n):
            return nc.alloc_semaphore(f"{name}_{n}")

        ident_in, = consts
        ident = sb("ident", [P, P])
        wr = sb("wr", [P, NC, E])
        xg = [sb(f"x{u}", [P, TG, D]) for u in range(2)]
        xn = [sb(f"xn{u}", [P, TG, D]) for u in range(2)]
        xt = [sb(f"xt{u}", [P, NC, GT]) for u in range(2)]
        stats = [sb(f"stats{u}", [P, TG, 6]) for u in range(2)]
        mv = [sb(f"mv{u}", [P, TG, 2]) for u in range(2)]
        ve = [sb(f"ve{u}", [P, TG]) for u in range(2)]
        sd = [sb(f"sd{u}", [P, TG]) for u in range(2)]
        r0 = [sb(f"r0{u}", [P, TG]) for u in range(2)]
        r1 = [sb(f"r1{u}", [P, TG]) for u in range(2)]
        rs = [sb(f"rs{u}", [P, TG]) for u in range(2)]
        pT = [ctx.enter_context(nc.psum_tensor(f"{name}_pT{k}", [P, GT], F32)) for k in range(2 * NC)]
        pL = [ctx.enter_context(nc.psum_tensor(f"{name}_pL{u}", [P, GT], F32)) for u in range(2)]

        s_const = sem("const")
        s_x = [sem(f"x{u}") for u in range(2)]
        s_st = [sem(f"st{u}") for u in range(2)]
        s_ch = sem("chain")
        s_ve = sem("ve")
        s_sd = sem("sd")
        s_xn = sem("xn")
        s_tr = sem("tr")
        s_xt = sem("xt")
        s_lg = sem("lg")
        s_lc = sem("lc")
        s_tick = sem("tick")
        AHEAD = 2

        with nc.Block() as block:
            @block.sync
            def _(sp):
                sp.dma_start(ident[:, :], ident_in).then_inc(s_const, DMA)
                if Wr is not None:
                    sp.dma_start(wr[:, :, :], Wr).then_inc(s_const, DMA)

                def load(g, u):
                    sp.wait_ge(s_xn, g + 1)
                    sp.dma_start(xg[u][:, :, :], x[bass.ds(g, 1), :, :, :].rearrange("g p i d -> p (g i) d"))\
                      .then_inc(s_x[u], DMA)

                def store(g, u):
                    sp.wait_ge(s_xt, g + (1 + AHEAD))
                    sp.dma_start(xnT[bass.ds(g, 1), :, :, :].rearrange("g p c t -> p (g c) t"),
                                 xt[u][:, :, :]).then_inc(s_st[u], DMA)

                stream(sp, load, store, [(s_st, 1)])

            @block.vector
            def _(ve_):
                ve_.sem_inc(s_xn, AHEAD)
                if Wr is not None:
                    ve_.sem_inc(s_lc, AHEAD)
                with ve_.Fori(0, NG // 2) as it:
                    ch = Chain(ve_, s_ch, 2 * (2 + 5), it)
                    for u in range(2):
                        ve_.wait_ge(s_x[u], it * DMA + DMA)
                        for i in range(TG):
                            last = ve_.bn_stats(stats[u][:, i, :], xg[u][:, i, :])
                        ch.add(last)
                        hold(ve_, s_ch, ch.base + ch.n, s_tick)
                        for i in range(TG):
                            last = ve_.bn_aggr(mv[u][:, i, :], stats[u][:, i, :])
                        ch.step(last)
                        ve_.tensor_scalar(ve[u][:, :], mv[u][:, :, 1], EPS, None, ALU.add).then_inc(s_ve, 1)
                    for u in range(2):
                        ve_.wait_ge(s_sd, it * 2 + (u + 1))
                        ch.step(ve_.reciprocal(r0[u][:, :], sd[u][:, :]))
                        ch.step(ve_.tensor_tensor(r1[u][:, :], r0[u][:, :], r0[u][:, :], ALU.mult))
                        ch.step(ve_.tensor_tensor(rs[u][:, :], r1[u][:, :], ve[u][:, :], ALU.mult))
                        ch.step(ve_.tensor_scalar(r1[u][:, :], rs[u][:, :], -0.5, 1.5, ALU.mult, ALU.add))
                        ch.step(ve_.tensor_tensor(rs[u][:, :], r0[u][:, :], r1[u][:, :], ALU.mult))
                        ve_.wait_ge(s_tr, it * 2 + (u + 1))
                        for i in range(TG):
                            last = ve_.tensor_scalar(xn[u][:, i, :], xg[u][:, i, :], mv[u][:, i, 0:1],
                                                     rs[u][:, i:i + 1], ALU.subtract, ALU.mult)
                        last.then_inc(s_xn, 1)
                    if Wr is not None:
                        for u in range(2):
                            ve_.wait_ge(s_lg, it * 2 + (u + 1))
                            ve_.tensor_copy(logits[:, bass.ds(it * (2 * TG * E) + u * TG * E, TG * E)],
                                            pL[u][:, 0:TG * E]).then_inc(s_lc, 1)
                    ch.close()

            @block.scalar
            def _(ac):
                ac.sem_inc(s_xt, AHEAD)
                for u in range(2):
                    ac.sem_inc(s_st[u], DMA)
                with ac.Fori(0, NG // 2) as it:
                    for u in range(2):
                        ac.wait_ge(s_ve, it * 2 + (u + 1))
                        ac.activation(sd[u][:, :], ve[u][:, :], ACT.Sqrt).then_inc(s_sd, 1)
                    for u in range(2):
                        ac.wait_ge(s_tr, it * 2 + (u + 1 + AHEAD))
                        ac.wait_ge(s_st[u], it * DMA + DMA)
                        if Wr is not None:
                            ac.wait_ge(s_lc, it * 2 + (u + 1))
                        for c in range(NC):
                            last = ac.activation(xt[u][:, c, :], pT[NC * u + c][:, :], ACT.Copy)
                        last.then_inc(s_xt, 1)

            @block.tensor
            def _(pe):
                pe.sem_inc(s_tr, AHEAD)
                pe.wait_ge(s_const, DMA * (2 if Wr is not None else 1))
                with pe.Fori(0, NG // 2) as it:
                    for u in range(2):
                        pe.wait_ge(s_xn, it * 2 + (u + 1 + AHEAD))
                        pe.wait_ge(s_xt, it * 2 + (u + 1))
                        for c in range(NC):
                            for i in range(TG):
                                last = pe.transpose(pT[NC * u + c][:, i * P:(i + 1) * P],
                                                    xn[u][:, i, c * P:(c + 1) * P], ident[:, :])
                        last.then_inc(s_tr, 1)
                    if Wr is not None:
                        for u in range(2):
                            pe.wait_ge(s_xt, it * 2 + (u + 1 + AHEAD))
                            for i in range(TG):
                                for c in range(NC):
                                    last = pe.matmul(pL[u][:, i * E:(i + 1) * E],
                                                     xt[u][:, c, i * P:(i + 1) * P], wr[:, c, :],
                                                     start=(c == 0), stop=(c == NC - 1))
                            last.then_inc(s_lg, 1)


def route_phase(nc, name, logits, weight, consts):
    before_in, order_in = consts
    with ExitStack() as ctx:
        def sb(n, shape, dt=F32):
            return ctx.enter_context(nc.sbuf_tensor(f"{name}_{n}", shape, dt))

        N = NT * E
        before32 = sb("before32", [P, P])
        before = sb("before", [P, P], BF16)
        ones = sb("ones", [P, P], BF16)
        ones32 = sb("ones32", [P, NT])
        order = sb("order", [P, E])
        t1, t2 = sb("t1", [P, NT, E]), sb("t2", [P, NT, E])
        sel = [sb(f"sel{k}", [P, NT, E]) for k in range(TOPK)]
        top = [sb(f"top{k}", [P, NT]) for k in range(TOPK)]
        rank = sb("rank", [P, NT])
        wk = [sb(f"wk{k}", [P, NT]) for k in range(TOPK)]
        gap, den = sb("gap", [P, NT]), sb("den", [P, NT])
        chosen = sb("chosen", [P, NT, E], BF16)
        count = sb("count", [P, NT, E])
        upto = sb("upto", [P, NT, E])
        p_in = ctx.enter_context(nc.psum_tensor(f"{name}_p_in", [P, N], F32))
        p_all = ctx.enter_context(nc.psum_tensor(f"{name}_p_all", [P, N], F32))
        s_c, s_ch, s_g, s_e, s_ma, s_mm = (nc.alloc_semaphore(f"{name}_{n}")
                                           for n in ("const", "chain", "gap", "exp", "mask", "sums"))
        L = logits[:, :].rearrange("p (t e) -> p t e", e=E)

        def over_e(ap):
            return ap.unsqueeze(2).to_broadcast([P, NT, E])

        with nc.Block() as block:
            @block.sync
            def _(sp):
                sp.dma_start(before32[:, :], before_in).then_inc(s_c, DMA)
                sp.dma_start(order[:, :], order_in).then_inc(s_c, DMA)

            @block.vector
            def _(ve):
                ch = Chain(ve, s_ch, None, None)
                ve.memset(ones32[:, :], 1.0)
                ch.step(ve.memset(ones[:, :], 1.0))
                ve.wait_ge(s_c, 2 * DMA)
                ch.step(ve.tensor_copy(before[:, :], before32[:, :]))
                left = L
                for k in range(TOPK):
                    ch.step(ve.tensor_reduce(out=top[k][:, :], in_=left, op=ALU.max, axis=AX.X))
                    ch.step(ve.tensor_tensor(t1[:, :, :], left, over_e(top[k][:, :]), ALU.is_ge))
                    ch.step(ve.tensor_tensor(t2[:, :, :], t1[:, :, :],
                                             order[:, :].unsqueeze(1).to_broadcast([P, NT, E]), ALU.mult))
                    ch.step(ve.tensor_reduce(out=rank[:, :], in_=t2[:, :, :], op=ALU.max, axis=AX.X))
                    ch.step(ve.tensor_tensor(sel[k][:, :, :], t2[:, :, :], over_e(rank[:, :]), ALU.is_equal))
                    if k == 0:
                        ch.step(ve.scalar_tensor_tensor(out=upto[:, :, :], in0=sel[0][:, :, :], scalar=-3e38,
                                                        in1=L, op0=ALU.mult, op1=ALU.add))
                        left = upto[:, :, :]
                ch.step(ve.tensor_tensor(chosen[:, :, :], sel[0][:, :, :], sel[1][:, :, :], ALU.add))
                ve.sem_inc(s_ma, 1)
                ve.tensor_tensor(gap[:, :], top[1][:, :], top[0][:, :], ALU.subtract).then_inc(s_g, 1)
                ve.wait_ge(s_e, 1)
                ch.step(ve.tensor_scalar(den[:, :], wk[1][:, :], 1.0, None, ALU.add))
                ch.step(ve.reciprocal(wk[0][:, :], den[:, :]))
                ch.step(ve.tensor_tensor(gap[:, :], wk[1][:, :], wk[0][:, :], ALU.mult))
                ch.step(ve.tensor_tensor(t1[:, :, :], sel[0][:, :, :], over_e(wk[0][:, :]), ALU.mult))
                ch.step(ve.tensor_tensor(t2[:, :, :], sel[1][:, :, :], over_e(gap[:, :]), ALU.mult))
                ch.step(ve.tensor_tensor(sel[0][:, :, :], t1[:, :, :], t2[:, :, :], ALU.add))
                ve.wait_ge(s_mm, 1)
                ch.step(ve.tensor_copy(count[:, :, :].rearrange("p t e -> p (t e)"), p_all[:, :]))
                for b in range(B):
                    for e in range(E):
                        ts = slice(b * NT // B, (b + 1) * NT // B)
                        ve_last = ve.tensor_tensor_scan(out=upto[:, ts, e], data0=ones32[:, ts],
                                                        data1=count[:, ts, e], initial=0.0,
                                                        op0=ALU.mult, op1=ALU.add)
                ch.step(ve_last)
                ch.step(ve.tensor_tensor(t1[:, :, :], upto[:, :, :], count[:, :, :], ALU.subtract))
                ch.step(ve.tensor_tensor(t2[:, :, :].rearrange("p t e -> p (t e)"),
                                         t1[:, :, :].rearrange("p t e -> p (t e)"), p_in[:, :], ALU.add))
                ch.step(ve.tensor_scalar(t1[:, :, :], t2[:, :, :], float(CAP), 0.5, ALU.is_lt, ALU.mult))
                ch.step(ve.tensor_tensor(weight[:, :, :], t1[:, :, :], sel[0][:, :, :], ALU.mult))

            @block.scalar
            def _(ac):
                ac.wait_ge(s_g, 1)
                ac.activation(wk[1][:, :], gap[:, :], ACT.Exp).then_inc(s_e, 1)

            @block.tensor
            def _(pe):
                pe.wait_ge(s_ma, 1)
                ch_flat = chosen[:, :, :].rearrange("p t e -> p (t e)")
                pe.matmul(p_in[:, :], before[:, :], ch_flat, start=True, stop=True)
                pe.matmul(p_all[:, :], ones[:, :], ch_flat, start=True, stop=True).then_inc(s_mm, 1)


def expert_phase(nc, name, x, xnT, We, weight, out):
    EP = 2
    with ExitStack() as ctx:
        def sb(n, shape, dt=F32):
            return ctx.enter_context(nc.sbuf_tensor(f"{name}_{n}", shape, dt))

        def sem(n):
            return nc.alloc_semaphore(f"{name}_{n}")

        we = sb("we", [P, NC, E, D])
        xt = [sb(f"xt{u}", [P, NC, GT]) for u in range(2)]
        xg = [sb(f"x{u}", [P, TG, D]) for u in range(2)]
        acc = [sb(f"acc{u}", [P, TG, D]) for u in range(2)]
        acb = [sb(f"acb{u}", [P, TG, D]) for u in range(2)]
        wg = [sb(f"wg{u}", [P, TG, E]) for u in range(2)]
        ps = [ctx.enter_context(nc.psum_tensor(f"{name}_ps{k}", [P, EP * D], F32)) for k in range(8)]
        s_we = sem("we")
        s_xt = [sem(f"xt{u}") for u in range(2)]
        s_x = [sem(f"x{u}") for u in range(2)]
        s_st = [sem(f"st{u}") for u in range(2)]
        s_mm = sem("mm")
        s_ac = sem("acc")
        NP = E // EP
        PAIRS = TG * NP
        STEPS = TG * E
        BANKS = len(ps)

        with nc.Block() as block:
            @block.sync
            def _(sp):
                sp.dma_start(we[:, :, :, :], We).then_inc(s_we, DMA)

                def load(g, u):
                    sp.wait_ge(s_ac, g * STEPS + STEPS)
                    sp.dma_start(xt[u][:, :, :], xnT[bass.ds(g, 1), :, :, :].rearrange("g p c t -> p (g c) t"))\
                      .then_inc(s_xt[u], DMA)
                    sp.dma_start(xg[u][:, :, :], x[bass.ds(g, 1), :, :, :].rearrange("g p i d -> p (g i) d"))\
                      .then_inc(s_x[u], DMA)

                def store(g, u):
                    sp.wait_ge(s_ac, g * STEPS + 3 * STEPS)
                    sp.dma_start(out[bass.ds(g, 1), :, :, :].rearrange("g p i d -> p (g i) d"),
                                 acc[u][:, :, :]).then_inc(s_st[u], DMA)

                stream(sp, load, store, [(s_st, 1)])

            @block.tensor
            def _(pe):
                pe.wait_ge(s_we, DMA)
                with pe.Fori(0, NG // 2) as it:
                    for u in range(2):
                        pe.wait_ge(s_xt[u], it * DMA + DMA)
                        for i in range(TG):
                            pe.wait_ge(s_ac, it * (2 * STEPS) + ((u + 2) * STEPS + (i - 1) * E))
                            for k in range(NP):
                                for c in range(NC):
                                    last = pe.matmul(ps[(i % 2) * NP + k][:, :],
                                                     xt[u][:, c, i * P:(i + 1) * P],
                                                     we[:, c, EP * k:EP * k + EP, :].rearrange("p e f -> p (e f)"),
                                                     start=(c == 0), stop=(c == NC - 1))
                                last.then_inc(s_mm, 1)

            @block.vector
            def _(ve):
                ve.sem_inc(s_ac, 2 * STEPS)
                for u in range(2):
                    ve.sem_inc(s_st[u], DMA)
                with ve.Fori(0, NG // 2) as it:
                    ve_base = it * (2 * STEPS)
                    for u in range(2):
                        ve.wait_ge(s_x[u], it * DMA + DMA)
                        ve.wait_ge(s_st[u], it * DMA + DMA)
                        for i in range(TG):
                            for e in range(E):
                                n = u * STEPS + i * E + e
                                if e % EP == 0:
                                    ve.wait_ge(s_mm, it * (2 * PAIRS) + (u * PAIRS + i * NP + e // EP + 1))
                                if e:
                                    ve.wait_ge(s_ac, ve_base + (2 * STEPS + n))
                                src = xg if e == 0 else (acb, acc)[(e - 1) % 2]
                                dst = (acb, acc)[e % 2]
                                ve.scalar_tensor_tensor(
                                    out=dst[u][:, i, :],
                                    in0=ps[(i % 2) * NP + e // EP][:, (e % EP) * D:(e % EP + 1) * D],
                                    scalar=weight[:, bass.ds(it * (2 * TG) + u * TG + i, 1), e],
                                    in1=src[u][:, i, :], op0=ALU.mult, op1=ALU.add).then_inc(s_ac, 1)


def qkv_phase(nc, name, xnT, wts, biases, tables, parts, v_out):
    wqk_in, wv_in = wts
    bqk_in, bv_in = biases
    cos_in, sin_in = tables
    with ExitStack() as ctx:
        def sb(n, shape, dt=F32):
            return ctx.enter_context(nc.sbuf_tensor(f"{name}_{n}", shape, dt))

        def sem(n):
            return nc.alloc_semaphore(f"{name}_{n}")

        wqk, wv = sb("wqk", [P, NC, 4, P]), sb("wv", [P, NC, D])
        bqk, bv, bs = sb("bqk", [P, 4]), sb("bv", [P, D]), sb("bs", [P, 4])
        xt = [sb(f"xt{u}", [P, NC, GT]) for u in range(2)]
        cs = [sb(f"cs{u}", [P, 2, GT]) for u in range(2)]
        ev, od = sb("even", [P, 2, GT]), sb("odd", [P, 2, GT])
        ec, es, oc, os_ = (sb(n, [P, 2, GT]) for n in ("ec", "es", "oc", "os"))
        rot = sb("rot", [P, 2, 2, GT])
        r1, r2 = sb("rest1", [P, 2, 2, GT]), sb("rest2", [P, 2, 2, GT])
        pt = [[sb(f"part{n}{u}", [P, 2, 2, GT], BF16) for n in range(3)] for u in range(2)]
        vt = [sb(f"v{u}", [P, H, TG, HD]) for u in range(2)]
        pqk = [ctx.enter_context(nc.psum_tensor(f"{name}_pqk{k}", [P, GT], F32)) for k in range(4)]
        pv = [ctx.enter_context(nc.psum_tensor(f"{name}_pv{k}", [P, 2 * D], F32)) for k in range(4)]

        s_c = sem("const")
        s_bs = sem("bs")
        s_xt = [sem(f"xt{u}") for u in range(2)]
        s_cs = [sem(f"cs{u}") for u in range(2)]
        s_st = [sem(f"st{u}") for u in range(2)]
        s_sv = [sem(f"sv{u}") for u in range(2)]
        s_qk = sem("qk")
        s_v = sem("v")
        s_ev = sem("evac")
        s_vc = sem("vcopy")
        s_ch = sem("chain")
        s_po = sem("pool")
        s_r = sem("rot")
        s_hi = sem("hi")
        s_r1 = sem("r1")
        s_mi = sem("mid")
        s_lo = sem("lo")
        s_tick = sem("tick")
        N_PARTS = 3

        with nc.Block() as block:
            @block.sync
            def _(sp):
                for dst, src in ((wqk[:, :, :, :], wqk_in), (wv[:, :, :], wv_in), (bqk[:, :], bqk_in),
                                 (bv[:, :], bv_in)):
                    sp.dma_start(dst, src).then_inc(s_c, DMA)

                def load(g, u):
                    sp.wait_ge(s_lo, g + 1)
                    sp.dma_start(xt[u][:, :, :], xnT[bass.ds(g, 1), :, :, :].rearrange("g p c t -> p (g c) t"))\
                      .then_inc(s_xt[u], DMA)
                    for k, tab in enumerate((cos_in, sin_in)):
                        sp.dma_start(cs[u][:, k:k + 1, :], tab[:, bass.ds(g, 1), :]).then_inc(s_cs[u], DMA)

                def store(g, u):
                    hold(sp, s_vc, g + 3, s_tick)
                    sp.dma_start(v_out[:, :, bass.ds(g, 1), :].rearrange("p h g n -> p h (g n)"),
                                 vt[u][:, :, :, :].rearrange("p h i d -> p h (i d)")).then_inc(s_sv[u], DMA)
                    hold(sp, s_lo, g + 3, s_tick)
                    for n in range(N_PARTS):
                        for half in range(2):
                            for w in range(2):
                                sp.dma_start(
                                    parts[w][n, half, :, bass.ds(g, 1), :].rearrange("p g t -> p (g t)"),
                                    pt[u][n][:, half, w, :]).then_inc(s_st[u], DMA)

                stream(sp, load, store, [(s_st, 4 * N_PARTS), (s_sv, 1)])

            @block.tensor
            def _(pe):
                pe.wait_ge(s_c, 4 * DMA)
                with pe.Fori(0, NG // 2) as it:
                    for u in range(2):
                        pe.wait_ge(s_xt[u], it * DMA + DMA)
                        pe.wait_ge(s_ev, it * 2 + (u + 1))
                        for m in range(4):
                            for c in range(NC):
                                last = pe.matmul(pqk[m][:, :], wqk[:, c, m, :], xt[u][:, c, :],
                                                 start=(c == 0), stop=(c == NC - 1))
                        last.then_inc(s_qk, 1)
                        pe.wait_ge(s_vc, it * 2 + (u + 1))
                        for i in range(TG):
                            for c in range(NC):
                                last = pe.matmul(pv[2 * u + i // 2][:, (i % 2) * D:(i % 2 + 1) * D],
                                                 xt[u][:, c, i * P:(i + 1) * P], wv[:, c, :],
                                                 start=(c == 0), stop=(c == NC - 1))
                        last.then_inc(s_v, 1)

            @block.scalar
            def _(ac):
                ac.sem_inc(s_ev, 1)
                ac.wait_ge(s_c, 4 * DMA)
                ac.activation(bs[:, 0:2], bqk[:, 0:2], ACT.Copy, scale=SCALE)
                ac.activation(bs[:, 2:4], bqk[:, 2:4], ACT.Copy).then_inc(s_bs, 1)
                ac.wait_ge(s_bs, 1)
                with ac.Fori(0, NG // 2) as it:
                    for u in range(2):
                        ac.wait_ge(s_qk, it * 2 + (u + 1))
                        ac.wait_ge(s_r, it * 2 + (u + 1))
                        for m in range(4):
                            dst = (ev, od)[m % 2]
                            last = ac.activation(dst[:, m // 2, :], pqk[m][:, :], ACT.Identity,
                                                 bias=bs[:, m:m + 1], scale=SCALE if m < 2 else 1.0)
                        last.then_inc(s_ev, 1)
                        ac.wait_ge(s_st[u], it * (3 * 4 * DMA) + DMA)
                        ac.wait_ge(s_r, it * 2 + (u + 2))
                        ac.activation(pt[u][0][:, :, :, :], rot[:, :, :, :], ACT.Copy).then_inc(s_hi, 1)
                        ac.wait_ge(s_r1, it * 2 + (u + 1))
                        ac.activation(pt[u][1][:, :, :, :], r1[:, :, :, :], ACT.Copy).then_inc(s_mi, 1)

            @block.vector
            def _(ve):
                ve.sem_inc(s_r, 1)
                ve.sem_inc(s_vc, 2)
                ve.sem_inc(s_lo, 2)
                for u in range(2):
                    ve.sem_inc(s_st[u], DMA)
                    ve.sem_inc(s_sv[u], DMA)
                ve.wait_ge(s_c, 4 * DMA)
                with ve.Fori(0, NG // 2) as it:
                    ch = Chain(ve, s_ch, 2, it)
                    for u in range(2):
                        cos = cs[u][:, 0:1, :].to_broadcast([P, 2, GT])
                        sin = cs[u][:, 1:2, :].to_broadcast([P, 2, GT])
                        ve.wait_ge(s_cs[u], it * (2 * DMA) + 2 * DMA)
                        ve.wait_ge(s_ev, it * 2 + (u + 2))
                        ve.tensor_tensor(ec[:, :, :], ev[:, :, :], cos, ALU.mult)
                        ch.step(ve.tensor_tensor(os_[:, :, :], od[:, :, :], sin, ALU.mult))
                        ve.tensor_tensor(rot[:, 0, :, :], ec[:, :, :], os_[:, :, :], ALU.subtract)
                        ve.wait_ge(s_po, it * 2 + (u + 1))
                        ve.tensor_tensor(rot[:, 1, :, :], es[:, :, :], oc[:, :, :], ALU.add).then_inc(s_r, 1)
                        ve.wait_ge(s_v, it * 2 + (u + 1))
                        ve.wait_ge(s_sv[u], it * DMA + DMA)
                        for i in range(TG):
                            last = ve.tensor_tensor(
                                vt[u][:, :, i, :],
                                pv[2 * u + i // 2][:, (i % 2) * D:(i % 2 + 1) * D].rearrange("p (h d) -> p h d", d=HD),
                                bv[:, :].rearrange("p (h d) -> p h d", d=HD), ALU.add)
                        last.then_inc(s_vc, 1)
                        ve.wait_ge(s_hi, it * 2 + (u + 1))
                        ve.tensor_tensor(r1[:, :, :, :], rot[:, :, :, :], pt[u][0][:, :, :, :],
                                         ALU.subtract).then_inc(s_r1, 1)
                        ve.wait_ge(s_mi, it * 2 + (u + 1))
                        ve.tensor_tensor(pt[u][2][:, :, :, :], r1[:, :, :, :], pt[u][1][:, :, :, :],
                                         ALU.subtract).then_inc(s_lo, 1)
                    ch.close()

            @block.gpsimd
            def _(gp):
                with gp.Fori(0, NG // 2) as it:
                    for u in range(2):
                        cos = cs[u][:, 0:1, :].to_broadcast([P, 2, GT])
                        sin = cs[u][:, 1:2, :].to_broadcast([P, 2, GT])
                        gp.wait_ge(s_cs[u], it * (2 * DMA) + 2 * DMA)
                        gp.wait_ge(s_ev, it * 2 + (u + 2))
                        gp.wait_ge(s_r, it * 2 + (u + 1))
                        gp.tensor_tensor(es[:, :, :], ev[:, :, :], sin, ALU.mult)
                        gp.tensor_tensor(oc[:, :, :], od[:, :, :], cos, ALU.mult).then_inc(s_po, 1)


def attend_phase(nc, name, parts, v_in, A, consts, rows_dram):
    q_parts, k_parts = parts
    fold_in, = consts
    NH = B * H
    QB = 512
    SB = S // QB
    KT = S // P
    TQ = QB // P
    KC = 2
    TERMS = [(0, 0), (0, 1), (0, 2), (1, 0), (1, 1), (2, 0)]
    ROWS = HD * len(TERMS)
    NB = 3
    NS = 3
    QUAD = 4
    NQ = KT // QUAD
    NX = 4
    FOLD_AT = 2 * QUAD
    SLOTS = KT + 1
    PAIRS = TQ * S // (QB * KC)
    XT = PAIRS * KC // NQ
    W = 32
    CH = 6
    assert SLOTS % NS == 0 and NQ % NX == 0 and 3 * TQ <= 32
    with ExitStack() as ctx:
        def sb(n, shape, dt=F32):
            return ctx.enter_context(nc.sbuf_tensor(f"{name}_{n}", shape, dt))

        def sem(n):
            return nc.alloc_semaphore(f"{name}_{n}")

        Q = [sb(f"q{p}", [P, S], BF16) for p in range(NB)]
        K = [sb(f"k{p}", [P, S], BF16) for p in range(NB)]
        vst = [sb(f"vst{p}", [P, KT, HD]) for p in range(NB)]
        V = [sb(f"v{p}", [P, KT, W]) for p in range(NB)]
        Ex = [sb(f"ex{j}", [P, QB]) for j in range(NX * QUAD)]
        O = sb("o", [P, QB])
        F = sb("f", [P, TQ, HD + 1])
        fold = sb("fold", [P, HD + 1])
        mx = sb("mx", [P, TQ, PAIRS // TQ])
        nm, rest, rest2 = sb("nm", [P, TQ]), sb("rest", [P, TQ]), sb("rest2", [P, TQ])
        m3 = sb("m3", [P, 32], BF16)
        m3T = sb("m3T", [P, 32], BF16)
        rec = sb("rec", [P, TQ, 1])
        ps = [ctx.enter_context(nc.psum_tensor(f"{name}_s{k}", [P, QB], F32)) for k in range(NS)]
        pm = [ctx.enter_context(nc.psum_tensor(f"{name}_m{k}", [P, KC * QB], F32)) for k in range(2)]
        po = ctx.enter_context(nc.psum_tensor(f"{name}_po", [P, QB], F32))
        fin = ps[FOLD_AT % NS][:, 0:TQ * (HD + 1)].rearrange("p (i d) -> p i d", d=HD + 1)

        s_c = sem("const")
        s_ld = [sem(f"load{p}") for p in range(NB)]
        s_lv = [sem(f"loadv{p}") for p in range(NB)]
        s_vh = sem("vh")
        s_one = sem("ones")
        s_kone = sem("kones")
        s_s = sem("scores")
        s_e = sem("exp")
        s_pv = sem("pv")
        s_m = sem("mtile")
        s_mr = sem("mred")
        s_ch = sem("chain")
        s_m3 = sem("m3")
        s_row = sem("rowout")
        s_mq = sem("mq")
        s_o = sem("o")
        s_f = sem("fold")
        s_a = sem("a")
        s_rc = sem("rec")
        s_tick = sem("tick")
        LOADS = 2 * len(TERMS)

        def slot(j):
            return j if j < FOLD_AT else j + 1

        def load(sp, p, h):
            for t, (a, b) in enumerate(TERMS):
                rows = slice(HD * t, HD * (t + 1))
                for dst, src in ((Q[p][rows, :], q_parts[a]), (K[p][rows, :], k_parts[b])):
                    sp.dma_start(dst, src[:, bass.ds(h, 1), :].rearrange("r h s -> r (h s)"))\
                      .then_inc(s_ld[p], DMA)
            sp.dma_start(vst[p][:, :, :],
                         v_in[:, bass.ds(h, 1), :].rearrange("p h n -> p (h n)").rearrange("p (k d) -> p k d", d=HD))\
              .then_inc(s_lv[p], DMA)

        def heads(eng, step):
            full = (NH - 2) // NB
            assert full * NB == NH - 2
            with eng.Fori(0, full) as n:
                for r in range(NB):
                    step(r, n * NB + r, n, True, True)
            step(0, NH - 2, full, True, False)
            step(1, NH - 1, full, False, False)

        with nc.Block() as block:
            @block.sync
            def _(sp):
                sp.dma_start(fold[:, :], fold_in).then_inc(s_c, DMA)
                load(sp, 0, 0)
                load(sp, 1, 1)

                def rows_of_max(p, h):
                    with sp.Fori(0, SB) as sb_:
                        w = h * SB + sb_
                        hold(sp, s_m3, w + 3, s_tick)
                        sp.dma_start(rows_dram[bass.ds(w, 1), :, :].rearrange("w p r -> p (w r)"), m3T[:, :])\
                          .then_inc(s_row, DMA)
                        hold(sp, s_row, w * DMA + 3 * DMA, s_tick)
                        src = rows_dram[bass.ds(w, 1), :, :].rearrange("w (b c) r -> b (w c) r", b=4)
                        for k in range(3):
                            sp.dma_start(
                                Q[p][ROWS + k:ROWS + k + 1, bass.ds(sb_ * QB, QB)]
                                .rearrange("p (i b r) -> p i b r", b=4, r=32),
                                src[:, TQ * k:TQ * (k + 1), :].rearrange("b i r -> i b r").unsqueeze(0))\
                              .then_inc(s_mq, DMA)
                        hold(sp, s_mq, w * (3 * DMA) + 3 * DMA, s_tick)

                rows_of_max(0, 0)

                def step(r, h, n, find, loads):
                    if loads:
                        hold(sp, s_pv, h * (SB * NQ) + (NX - 1 + 1), s_tick)
                        hold(sp, s_vh, h + 1, s_tick)
                        load(sp, (r + 2) % NB, h + 2)
                    if find:
                        rows_of_max((r + 1) % NB, h + 1)

                heads(sp, step)

            @block.gpsimd
            def _(gp):
                for p in range(NB):
                    gp.memset(V[p][:, :, :], 0.0)
                for j in range(QUAD):
                    last = gp.memset(Ex[(NX - 1) * QUAD + j][:, :], 1.0)
                last.then_inc(s_one, 1)
                gp.wait_ge(s_one, 1)
                for p in range(NB):
                    last = gp.memset(V[p][:, :, HD:HD + 1], 1.0)
                last.then_inc(s_one, 1)
                gp.wait_ge(s_one, 2)

                def fill(p, n):
                    hold(gp, s_lv[p], n * DMA + DMA, s_tick)
                    gp.tensor_copy(V[p][:, :, 0:HD], vst[p][:, :, :]).then_inc(s_vh, 1)

                fill(0, 0)

                def step(r, h, n, find, loads):
                    if find:
                        gp.wait_ge(s_pv, h * (SB * NQ) + (NX - 1 + 1))
                        fill((r + 1) % NB, n + (r + 1) // NB)

                heads(gp, step)

            @block.tensor
            def _(pe):
                pe.sem_inc(s_pv, NX - 1)
                pe.sem_inc(s_f, 1)
                pe.wait_ge(s_c, DMA)
                pe.wait_ge(s_kone, 1)
                pe.wait_ge(s_one, 2)

                def max_chunk(k, p, sb_, w):
                    i, c = divmod(k, S // QB)
                    if c % KC == 0:
                        pe.wait_ge(s_mr, w * PAIRS + (k // KC + 1))
                    ins = pe.matmul(pm[(k // KC) % 2][:, (c % KC) * QB:(c % KC + 1) * QB],
                                    Q[p][0:ROWS, bass.ds(sb_ * QB + i * P, P)],
                                    K[p][0:ROWS, c * QB:(c + 1) * QB], start=True, stop=True)
                    if c % KC == KC - 1:
                        ins.then_inc(s_m, 1)

                def times_v(p, q):
                    for g in range(QUAD):
                        last = pe.matmul(po[W * g:W * (g + 1), :], V[p][:, QUAD * q + g, :],
                                         Ex[QUAD * (q % NX) + g][:, :], start=(q == 0), stop=(q == NQ - 1))
                    return last

                def fold_output(u):
                    pe.wait_ge(s_e, u * SLOTS + (FOLD_AT + 1))
                    pe.wait_ge(s_o, u + 1)
                    for i in range(TQ):
                        last = pe.matmul(fin[:, i, :], O[:, i * P:(i + 1) * P], fold[:, :],
                                         start=True, stop=True)
                    last.then_inc(s_f, 1)

                def unit(find, p, p_before, sb_, u):
                    w = u + SB
                    pe.wait_ge(s_mq, u * (3 * DMA) + 3 * DMA)
                    for q in range(NQ):
                        for k in range(QUAD):
                            j = q * QUAD + k
                            pe.wait_ge(s_e, u * SLOTS + (slot(j) + 1))
                            pe.matmul(ps[slot(j) % NS][:, :], K[p][0:ROWS + 3, j * P:(j + 1) * P],
                                      Q[p][0:ROWS + 3, bass.ds(sb_ * QB, QB)],
                                      start=True, stop=True).then_inc(s_s, 1)
                            if find:
                                for x in range(XT // QUAD):
                                    max_chunk(q * XT + k * (XT // QUAD) + x, (p + 1) % NB, sb_, w)
                        if q == 0:
                            pe.wait_ge(s_e, u * SLOTS + NS)
                            times_v(p_before, NQ - 1).then_inc(s_pv, 1)
                        else:
                            if q == 1:
                                fold_output(u)
                            pe.wait_ge(s_e, u * SLOTS + (slot(QUAD * q - 1) + 1 + NS))
                            times_v(p, q - 1).then_inc(s_pv, 1)

                for g in range(QUAD):
                    pe.matmul(po[W * g:W * (g + 1), :], V[NB - 1][:, 0, :], Ex[(NX - 1) * QUAD + g][:, :],
                              start=True, stop=False)
                pe.wait_ge(s_ld[0], LOADS * DMA)
                with pe.Fori(0, SB) as sb_:
                    for k in range(TQ * S // QB):
                        max_chunk(k, 0, sb_, sb_)

                def step(r, h, n, find, loads):
                    hold(pe, s_vh, h + 1, s_tick)
                    if find:
                        hold(pe, s_ld[(r + 1) % NB], (n + (r + 1) // NB) * (LOADS * DMA) + LOADS * DMA, s_tick)
                    unit(find, r, (r - 1) % NB, 0, h * SB)
                    with pe.Fori(1, SB) as sb_:
                        unit(find, r, r, sb_, h * SB + sb_)

                heads(pe, step)
                pe.wait_ge(s_e, NH * SB * SLOTS + NS)
                times_v((NH - 1) % NB, NQ - 1).then_inc(s_pv, 1)
                pe.wait_ge(s_o, NH * SB + 1)
                for i in range(TQ):
                    last = pe.matmul(fin[:, i, :], O[:, i * P:(i + 1) * P], fold[:, :], start=True, stop=True)
                last.then_inc(s_f, 1)

            @block.scalar
            def _(ac):
                ac.sem_inc(s_e, NS)

                def take_output(u):
                    ac.wait_ge(s_pv, u * NQ + (NX - 1 + 1))
                    ac.wait_ge(s_f, u + 1)
                    ac.activation(O[:, :], po[:, :], ACT.Copy).then_inc(s_o, 1)

                def take_folded(u):
                    ac.wait_ge(s_f, u + 2)
                    ac.wait_ge(s_a, u + 1)
                    return ac.activation(F[:, :, :], fin, ACT.Copy)

                def unit(u):
                    for j in range(KT):
                        if j % QUAD == 0:
                            ac.wait_ge(s_pv, u * NQ + (j // QUAD + 1))
                        ac.wait_ge(s_s, u * KT + (j + 1))
                        ac.activation(Ex[j % (NX * QUAD)][:, :], ps[slot(j) % NS][:, :], ACT.Exp)\
                          .then_inc(s_e, 1)
                        if j == QUAD - 1:
                            take_output(u)
                        if j == FOLD_AT - 1:
                            take_folded(u).then_inc(s_e, 1)

                def step(r, h, n, find, loads):
                    with ac.Fori(0, SB) as sb_:
                        unit(h * SB + sb_)

                heads(ac, step)
                take_output(NH * SB)
                take_folded(NH * SB).then_inc(s_e, 1)

            @block.vector
            def _(ve):
                ve.sem_inc(s_mr, 2)
                ve.sem_inc(s_a, 1)
                ve.sem_inc(s_m3, 1)
                ve.sem_inc(s_row, 2 * DMA)
                for p in range(NB):
                    last = ve.memset(K[p][ROWS:ROWS + 3, :], 1.0)
                last.then_inc(s_kone, 1)
                ve.memset(m3[:, :], 0.0)
                ve.memset(nm[:, :], 0.0).then_inc(s_ch, 1)

                def find_max(k, w):
                    if k == 0:
                        ve.wait_ge(s_ch, w * CH + 1)
                    ve.wait_ge(s_m, w * PAIRS + (k + 1))
                    per = PAIRS // TQ
                    ve.tensor_reduce(out=mx[:, k // per, k % per:k % per + 1], in_=pm[k % 2][:, :],
                                     op=ALU.max, axis=AX.X).then_inc(s_mr, 1)

                def split(n, w):
                    ve.wait_ge(s_ch, w * CH + (n + 1))
                    part = [m3[:, TQ * k:TQ * (k + 1)] for k in range(3)]
                    if n == 0:
                        ve.wait_ge(s_m3, w + 1)
                        ve.tensor_copy(part[0], nm[:, :]).then_inc(s_ch, 1)
                    if n == 1:
                        ve.tensor_tensor(rest[:, :], nm[:, :], part[0], ALU.subtract).then_inc(s_ch, 1)
                    if n == 2:
                        ve.tensor_copy(part[1], rest[:, :]).then_inc(s_ch, 1)
                    if n == 3:
                        ve.tensor_tensor(rest2[:, :], rest[:, :], part[1], ALU.subtract).then_inc(s_ch, 1)
                    if n == 4:
                        ve.tensor_copy(part[2], rest2[:, :]).then_inc(s_ch, 1)
                    if n == 5:
                        ve.wait_ge(s_row, w * DMA + DMA)
                        ve.transpose(m3T[:, :], m3[:, :]).then_inc(s_m3, 1)

                def normalise(n, u, at=FOLD_AT):
                    if n == 0:
                        ve.wait_ge(s_e, u * SLOTS + (at + 1 + NS))
                        ve.reciprocal(rec[:, :, :], F[:, :, HD:HD + 1]).then_inc(s_rc, 1)
                    else:
                        ve.wait_ge(s_rc, u + 1)
                        ve.tensor_tensor(A[:, bass.ds(u, 1), :, :].rearrange("p u i d -> p (u i) d"),
                                         F[:, :, 0:HD], rec[:, :, :].to_broadcast([P, TQ, HD]),
                                         ALU.mult).then_inc(s_a, 1)

                def unit(main, find, u, w):
                    for k in range(PAIRS):
                        if find:
                            find_max(k, w)
                            if k < CH:
                                split(k, w)
                        if main and k in (CH, CH + 1):
                            normalise(k - CH, u)
                    if find:
                        ve.wait_ge(s_mr, w * PAIRS + (PAIRS + 2))
                        ve.tensor_reduce(out=nm[:, :], in_=mx[:, :, :], op=ALU.max, axis=AX.X, negate=True)\
                          .then_inc(s_ch, 1)

                with ve.Fori(0, SB) as sb_:
                    unit(False, True, None, sb_)

                def step(r, h, n, find, loads):
                    if not find:
                        for k in range(CH):
                            split(k, NH * SB)
                    with ve.Fori(0, SB) as sb_:
                        unit(True, find, h * SB + sb_, (h + 1) * SB + sb_)

                heads(ve, step)
                for k in range(2):
                    normalise(k, NH * SB, 0)
                ve.wait_ge(s_a, NH * SB + 2)


def out_phase(nc, name, x, A, Wo, bo, consts, out):
    ident_in, = consts
    with ExitStack() as ctx:
        def sb(n, shape, dt=F32):
            return ctx.enter_context(nc.sbuf_tensor(f"{name}_{n}", shape, dt))

        def sem(n):
            return nc.alloc_semaphore(f"{name}_{n}")

        ident = sb("ident", [P, P])
        wo = sb("wo", [P, NC, D])
        bo_sb = sb("bo", [P, D])
        at = [sb(f"at{u}", [P, TG, D]) for u in range(2)]
        aT = [sb(f"aT{u}", [P, NC, GT]) for u in range(2)]
        xg = [sb(f"x{u}", [P, TG, D]) for u in range(2)]
        xb = [sb(f"xb{u}", [P, TG, D]) for u in range(2)]
        y = [sb(f"y{u}", [P, TG, D]) for u in range(2)]
        pT = [ctx.enter_context(nc.psum_tensor(f"{name}_pT{k}", [P, GT], F32)) for k in range(2 * NC)]
        py = [ctx.enter_context(nc.psum_tensor(f"{name}_py{k}", [P, 2 * D], F32)) for k in range(4)]
        s_c = sem("const")
        s_x = [sem(f"x{u}") for u in range(2)]
        s_st = [sem(f"st{u}") for u in range(2)]
        s_at = sem("at")
        s_tr = sem("tr")
        s_aT = sem("aT")
        s_y = sem("y")
        s_xb = sem("xb")
        s_o = sem("out")

        with nc.Block() as block:
            @block.sync
            def _(sp):
                for dst, src in ((ident[:, :], ident_in), (wo[:, :, :], Wo), (bo_sb[:, :], bo)):
                    sp.dma_start(dst, src).then_inc(s_c, DMA)

                def load(g, u):
                    sp.wait_ge(s_xb, g + 1)
                    sp.dma_start(xg[u][:, :, :], x[bass.ds(g, 1), :, :, :].rearrange("g p i d -> p (g i) d"))\
                      .then_inc(s_x[u], DMA)

                def store(g, u):
                    sp.wait_ge(s_o, g + 3)
                    sp.dma_start(out[bass.ds(g, 1), :, :, :].rearrange("g p i d -> p (g i) d"),
                                 y[u][:, :, :]).then_inc(s_st[u], DMA)

                stream(sp, load, store, [(s_st, 1)])

            @block.scalar
            def _(ac):
                ac.sem_inc(s_aT, 2)
                for b in range(B):
                    heads = A[:, 1:1 + H * B * GB, :, :].rearrange("p (h b s) i d -> p h b s i d", b=B, s=GB)
                    with ac.Fori(0, GB // 2) as it:
                        for u in range(2):
                            n = it * 2 + (b * GB + u)
                            ac.wait_ge(s_tr, n + 1)
                            for i in range(TG):
                                last = ac.activation(
                                    at[u][:, i, :].rearrange("p (h d) -> p h d", d=HD),
                                    heads[:, :, b, bass.ds(it * 2 + u, 1), i, :].rearrange("p h s d -> p h (s d)"),
                                    ACT.Copy)
                            last.then_inc(s_at, 1)
                        for u in range(2):
                            n = it * 2 + (b * GB + u)
                            ac.wait_ge(s_tr, n + 3)
                            ac.wait_ge(s_o, n + 1)
                            for c in range(NC):
                                last = ac.activation(aT[u][:, c, :], pT[NC * u + c][:, :], ACT.Copy)
                            last.then_inc(s_aT, 1)

            @block.tensor
            def _(pe):
                pe.sem_inc(s_tr, 2)
                pe.wait_ge(s_c, 3 * DMA)
                with pe.Fori(0, NG // 2) as it:
                    for u in range(2):
                        pe.wait_ge(s_at, it * 2 + (u + 1))
                        pe.wait_ge(s_aT, it * 2 + (u + 1))
                        for c in range(NC):
                            for i in range(TG):
                                last = pe.transpose(pT[NC * u + c][:, i * P:(i + 1) * P],
                                                    at[u][:, i, c * P:(c + 1) * P], ident[:, :])
                        last.then_inc(s_tr, 1)
                    for u in range(2):
                        pe.wait_ge(s_aT, it * 2 + (u + 3))
                        pe.wait_ge(s_o, it * 2 + (u + 1))
                        for i in range(TG):
                            for c in range(NC):
                                last = pe.matmul(py[2 * u + i // 2][:, (i % 2) * D:(i % 2 + 1) * D],
                                                 aT[u][:, c, i * P:(i + 1) * P], wo[:, c, :],
                                                 start=(c == 0), stop=(c == NC - 1))
                        last.then_inc(s_y, 1)

            @block.vector
            def _(ve):
                ve.sem_inc(s_xb, 2)
                ve.sem_inc(s_o, 2)
                for u in range(2):
                    ve.sem_inc(s_st[u], DMA)
                ve.wait_ge(s_c, 3 * DMA)
                with ve.Fori(0, NG // 2) as it:
                    for u in range(2):
                        ve.wait_ge(s_x[u], it * DMA + DMA)
                        for i in range(TG):
                            last = ve.tensor_tensor(xb[u][:, i, :], xg[u][:, i, :], bo_sb[:, :], ALU.add)
                        last.then_inc(s_xb, 1)
                    for u in range(2):
                        ve.wait_ge(s_y, it * 2 + (u + 1))
                        ve.wait_ge(s_xb, it * 2 + (u + 3))
                        ve.wait_ge(s_st[u], it * DMA + DMA)
                        for i in range(TG // 2):
                            last = ve.tensor_tensor(
                                y[u][:, 2 * i:2 * i + 2, :].rearrange("p i d -> p (i d)"), py[2 * u + i][:, :],
                                xb[u][:, 2 * i:2 * i + 2, :].rearrange("p i d -> p (i d)"), ALU.add)
                        last.then_inc(s_o, 1)


def program(nc, x, w, c, out):
    def grouped(ap):
        return ap.rearrange("(g i p) d -> g p i d", i=TG, p=P)

    def dram(n, shape, dt=F32):
        return nc.dram_tensor(n, shape, dt, kind="Internal").ap()

    x1 = dram("after_ffn1", (NG, P, TG, D))
    x2 = dram("after_attention", (NG, P, TG, D))
    xnT = dram("normalised", (NG, P, NC, GT))
    qk = [dram(f"{n}_parts", (3, 2, P, NG, GT), BF16) for n in "qk"]
    vd = dram("v_by_head", (P, H, NG, TG * HD))

    with ExitStack() as ctx:
        A = ctx.enter_context(nc.sbuf_tensor("attended", [P, 1 + B * H * GB, TG, HD], F32))
        logits = A[:, 0:NT * E // (TG * HD), :, :].rearrange("p u i d -> p (u i d)")
        weight = A[:, 64:64 + NT * E // (TG * HD), :, :].rearrange("p u i d -> p (u i d)")\
            .rearrange("p (t e) -> p t e", e=E)

        def moe(name, src, dst):
            norm_phase(nc, name + "n", src, xnT, (c["ident"],), w["Wr"], logits)
            route_phase(nc, name + "r", logits, weight, (c["before"], c["order"]))
            expert_phase(nc, name + "e", src, xnT, w["We"], weight, dst)

        moe("f1", grouped(x), x1)
        norm_phase(nc, "an", x1, xnT, (c["ident"],))
        qkv_phase(nc, "ap", xnT, (w["Wqk"], w["Wv"]), (w["bqk"], w["bv"]), (c["cos"], c["sin"]), qk, vd)
        attend_phase(nc, "at",
                     [[t[k].rearrange("f (j h) (b g) t -> (f j) (h b) (g t)", h=H, b=B) for k in range(3)] for t in qk],
                     vd.rearrange("p h (b g) n -> p (h b) (g n)", b=B), A, (c["fold"],),
                     dram("max_rows", (B * H * S // 512, P, 32), BF16))
        out_phase(nc, "ao", x1, A, w["Wo"], w["bo"], (c["ident"],), x2)
        moe("f2", x2, grouped(out))


def shape_constants():
    inv_freq = (np.float32(1.0) / np.float32(10000.0) ** (np.arange(0, HD, 2, dtype=np.float32) / np.float32(HD)))
    angle = np.arange(S, dtype=np.float32)[:, None] * inv_freq.astype(np.float32)[None, :]
    rows = np.repeat(np.arange(HD // 2), H)

    def table(f):
        t = f(angle).astype(np.float32)[:, rows].T.reshape(P, GB, GT)
        return np.ascontiguousarray(np.concatenate([t] * B, axis=1))

    fold = np.zeros((P, HD + 1), np.float32)
    for g in range(4):
        fold[32 * g:32 * g + HD + 1] = np.eye(HD + 1, dtype=np.float32)
    return {
        "ident": np.eye(P, dtype=np.float32),
        "before": np.triu(np.ones((P, P), np.float32), 1),
        "order": np.tile(np.arange(E, 0, -1, dtype=np.float32), (P, 1)),
        "fold": fold,
        "cos": table(np.cos),
        "sin": table(np.sin),
    }


def kernel(L0_attn_x, L0_attn_Wq, L0_attn_bq, L0_attn_Wk, L0_attn_bk, L0_attn_Wv, L0_attn_bv,
           L0_attn_Wo, L0_attn_bo, L0_ffn_Wr, L0_ffn_We):
    import concourse.bacc as bacc
    from concourse.bass_utils import run_bass_kernel_spmd

    def by_feature(a):
        return a.T.reshape(NC, P, -1).transpose(1, 0, 2)

    def halves(W):
        return [W.reshape(H, HD // 2, 2, -1)[:, :, k, :].transpose(1, 0, 2).reshape(P, -1) for k in range(2)]

    X = {n: np.asarray(a) for n, a in dict(
        x=L0_attn_x, Wq=L0_attn_Wq, bq=L0_attn_bq, Wk=L0_attn_Wk, bk=L0_attn_bk, Wv=L0_attn_Wv,
        bv=L0_attn_bv, Wo=L0_attn_Wo, bo=L0_attn_bo, Wr=L0_ffn_Wr, We=L0_ffn_We).items()}
    arrays = {
        "x": X["x"].reshape(B * S, D),
        "Wqk": np.stack([by_feature(m) for m in halves(X["Wq"]) + halves(X["Wk"])], axis=2),
        "bqk": np.concatenate(halves(X["bq"].reshape(D, 1)) + halves(X["bk"].reshape(D, 1)), axis=1),
        "Wv": by_feature(X["Wv"]),
        "bv": np.tile(X["bv"], (P, 1)),
        "Wo": by_feature(X["Wo"]),
        "bo": np.tile(X["bo"], (P, 1)),
        "Wr": by_feature(X["Wr"]),
        "We": X["We"].reshape(E, NC, P, D).transpose(2, 1, 0, 3),
    }
    consts = shape_constants()
    nc = bacc.Bacc("TRN2", target_bir_lowering=False, num_devices=1)
    given, aps = {}, {}
    for n, a in {**arrays, **{"c_" + k: v for k, v in consts.items()}}.items():
        given[f"in_{n}"] = np.ascontiguousarray(a)
        aps[n] = nc.dram_tensor(f"in_{n}", a.shape, F32, kind="ExternalInput").ap()
    out = nc.dram_tensor("out", (B * S, D), F32, kind="ExternalOutput").ap()
    program(nc, aps["x"], aps, {k: aps["c_" + k] for k in consts}, out)
    r = run_bass_kernel_spmd(nc, [given], core_ids=[0])
    return r.results[0]["out"].reshape(B, S, D)
```

```python
import concourse.bass as bass
import numpy as np
from concourse import mybir
from contextlib import ExitStack

F32 = mybir.dt.float32
BF16 = mybir.dt.bfloat16
ALU = mybir.AluOpType
ACT = mybir.ActivationFunctionType
AX = mybir.AxisListType

P = 128
B, S, D = 2, 4096, 256
H, HD = 16, 16
E, TOPK = 8, 2
CAP = int(S * TOPK / E * 1.5) + 1
EPS = 1e-5
NC = D // P
NT = B * S // P
TG = 4
GT = TG * P
NG = NT // TG
GB = NG // B
SCALE = HD ** -0.5
DMA = 16


def hold(eng, sem, value, tick):
    eng.wait_ge(sem, value)
    eng.sem_inc(tick, 1)


class Chain:

    def __init__(self, eng, sem, per_round, rounds_done):
        self.eng, self.sem, self.per_round, self.n = eng, sem, per_round, 0
        self.base = rounds_done * per_round if rounds_done is not None else 0

    def add(self, ins):
        self.n += 1
        ins.then_inc(self.sem, 1)

    def settle(self):
        self.eng.wait_ge(self.sem, self.base + self.n)

    def step(self, ins):
        self.add(ins)
        self.settle()

    def close(self):
        assert self.per_round is None or self.n == self.per_round, self.n


class NormBuffers:
    pass


def norm_buffers(nc, ctx, name, ident, xnT, wr=None, logits=None):
    def sb(n, shape, dt=F32):
        return [ctx.enter_context(nc.sbuf_tensor(f"{name}_{n}{u}", shape, dt)) for u in range(2)]

    def sem(n):
        return nc.alloc_semaphore(f"{name}_{n}")

    nm = NormBuffers()
    nm.ident, nm.xnT, nm.wr, nm.logits = ident, xnT, wr, logits
    nm.xn, nm.xt = sb("xn", [P, TG, D]), sb("xt", [P, NC, GT])
    nm.stats, nm.mv = sb("stats", [P, TG, 6]), sb("mv", [P, TG, 2])
    nm.var, nm.root_, nm.r0, nm.r1, nm.rs = (sb(n, [P, TG]) for n in ("var", "root", "r0", "r1", "rs"))
    nm.pT = [ctx.enter_context(nc.psum_tensor(f"{name}_pT{c}", [P, GT], F32)) for c in range(NC)]
    if wr is not None:
        nm.pL = ctx.enter_context(nc.psum_tensor(f"{name}_pL", [P, TG * E], F32))
    nm.s_st = [sem(f"st{u}") for u in range(2)]
    nm.s_a = sem("stats")
    nm.s_b = sem("newton")
    nm.s_var = sem("var")
    nm.s_root = sem("root")
    nm.s_xn = sem("xn")
    nm.s_tr = sem("tr")
    nm.s_xt = sem("xt")
    nm.s_lg = sem("lg")
    nm.s_lc = sem("lc")
    nm.s_tick = sem("tick")
    return nm


def norm_begin_vector(nm, ve):
    ve.sem_inc(nm.s_xn, 2)
    ve.sem_inc(nm.s_lc, 2)


def norm_begin_scalar(nm, ac):
    ac.sem_inc(nm.s_xt, 1)
    for u in range(2):
        ac.sem_inc(nm.s_st[u], DMA)


def norm_begin_tensor(nm, pe):
    pe.sem_inc(nm.s_tr, 2)


def norm_statistics(nm, ve, g, u, x):
    ve.wait_ge(nm.s_xn, g + 1)
    for i in range(TG):
        last = ve.bn_stats(nm.stats[u][:, i, :], x[:, i, :])
    last.then_inc(nm.s_a, 1)
    hold(ve, nm.s_a, g * 2 + 1, nm.s_tick)
    for i in range(TG):
        last = ve.bn_aggr(nm.mv[u][:, i, :], nm.stats[u][:, i, :])
    last.then_inc(nm.s_a, 1)
    ve.wait_ge(nm.s_a, g * 2 + 2)
    ve.tensor_scalar(nm.var[u][:, :], nm.mv[u][:, :, 1], EPS, None, ALU.add).then_inc(nm.s_var, 1)


def norm_root(nm, ac, g, u):
    ac.wait_ge(nm.s_var, g + 1)
    ac.activation(nm.root_[u][:, :], nm.var[u][:, :], ACT.Sqrt).then_inc(nm.s_root, 1)


def normalise(nm, ve, g, u, x):
    r0, r1, rs, var = nm.r0[u], nm.r1[u], nm.rs[u], nm.var[u]
    ve.wait_ge(nm.s_root, g + 1)
    ch = Chain(ve, nm.s_b, 5, g)
    ch.step(ve.reciprocal(r0[:, :], nm.root_[u][:, :]))
    ch.step(ve.tensor_tensor(r1[:, :], r0[:, :], r0[:, :], ALU.mult))
    ch.step(ve.tensor_tensor(rs[:, :], r1[:, :], var[:, :], ALU.mult))
    ch.step(ve.tensor_scalar(r1[:, :], rs[:, :], -0.5, 1.5, ALU.mult, ALU.add))
    ch.step(ve.tensor_tensor(rs[:, :], r0[:, :], r1[:, :], ALU.mult))
    ch.close()
    ve.wait_ge(nm.s_tr, g + 1)
    for i in range(TG):
        last = ve.tensor_scalar(nm.xn[u][:, i, :], x[:, i, :], nm.mv[u][:, i, 0:1],
                                rs[:, i:i + 1], ALU.subtract, ALU.mult)
    last.then_inc(nm.s_xn, 1)


def norm_turn(nm, pe, g, u):
    pe.wait_ge(nm.s_xn, g + 3)
    pe.wait_ge(nm.s_xt, g + 1)
    for c in range(NC):
        for i in range(TG):
            last = pe.transpose(nm.pT[c][:, i * P:(i + 1) * P],
                                nm.xn[u][:, i, c * P:(c + 1) * P], nm.ident[:, :])
    last.then_inc(nm.s_tr, 1)


def norm_turned(nm, ac, g, g_of_u, u):
    ac.wait_ge(nm.s_tr, g + 3)
    ac.wait_ge(nm.s_st[u], g_of_u * DMA + DMA)
    if nm.wr is not None:
        ac.wait_ge(nm.s_lc, g + 1)
    for c in range(NC):
        last = ac.activation(nm.xt[u][:, c, :], nm.pT[c][:, :], ACT.Copy)
    last.then_inc(nm.s_xt, 1)


def norm_route(nm, pe, g, u):
    pe.wait_ge(nm.s_xt, g + 2)
    pe.wait_ge(nm.s_lc, g + 2)
    for i in range(TG):
        for c in range(NC):
            last = pe.matmul(nm.pL[:, i * E:(i + 1) * E], nm.xt[u][:, c, i * P:(i + 1) * P],
                             nm.wr[:, c, :], start=(c == 0), stop=(c == NC - 1))
    last.then_inc(nm.s_lg, 1)


def norm_routed(nm, ve, g):
    ve.wait_ge(nm.s_lg, g + 1)
    ve.tensor_copy(nm.logits[:, bass.ds(g * (TG * E), TG * E)], nm.pL[:, :]).then_inc(nm.s_lc, 1)


def norm_store(nm, sp, g, u):
    sp.wait_ge(nm.s_xt, g + 2)
    sp.dma_start(nm.xnT[bass.ds(g, 1), :, :, :].rearrange("g p c t -> p (g c) t"),
                 nm.xt[u][:, :, :]).then_inc(nm.s_st[u], DMA)


def norm_stored(nm, sp):
    for u in range(2):
        sp.wait_ge(nm.s_st[u], DMA * (NG // 2 + 1))


def norm_settled(nm, ve):
    if nm.wr is not None:
        ve.wait_ge(nm.s_lc, NG + 2)


def norm_phase(nc, name, x, xnT, ident_in, Wr, logits):
    U = 4
    with ExitStack() as ctx:
        def sb(n, shape, dt=F32):
            return ctx.enter_context(nc.sbuf_tensor(f"{name}_{n}", shape, dt))

        def sem(n):
            return nc.alloc_semaphore(f"{name}_{n}")

        ident, wr = sb("ident", [P, P]), sb("wr", [P, NC, E])
        xg = [sb(f"x{u}", [P, TG, D]) for u in range(U)]
        s_c = sem("const")
        s_x = [sem(f"x{u}") for u in range(U)]
        nm = norm_buffers(nc, ctx, name + "_n", ident, xnT, wr, logits)

        with nc.Block() as block:
            @block.sync
            def _(sp):
                sp.dma_start(ident[:, :], ident_in).then_inc(s_c, DMA)
                sp.dma_start(wr[:, :, :], Wr).then_inc(s_c, DMA)

                def load(g, u):
                    sp.dma_start(xg[u][:, :, :], x[bass.ds(g, 1), :, :, :].rearrange("g p i d -> p (g i) d"))\
                      .then_inc(s_x[u], DMA)

                for u in range(U):
                    load(u, u)

                def body(g, u, more):
                    if more:
                        hold(sp, nm.s_xn, g + 3, nm.s_tick)
                        load(g + U, u)
                    norm_store(nm, sp, g, u % 2)

                with sp.Fori(0, NG // U - 1) as it:
                    for u in range(U):
                        body(it * U + u, u, True)
                for u in range(U):
                    body(NG - U + u, u, False)
                norm_stored(nm, sp)

            @block.vector
            def _(ve):
                norm_begin_vector(nm, ve)

                def stats(g, u, rounds):
                    ve.wait_ge(s_x[u], rounds * DMA + DMA)
                    norm_statistics(nm, ve, g, u % 2, xg[u])

                stats(0, 0, 0)

                def round_(it, first, last):
                    for u in range(U):
                        g = it * U + u
                        if not (last and u == U - 1):
                            stats(g + 1, (u + 1) % U, it + (u + 1) // U)
                        normalise(nm, ve, g, u % 2, xg[u])
                        if not (first and u == 0):
                            norm_routed(nm, ve, g - 1)

                round_(0, True, False)
                with ve.Fori(1, NG // U - 1) as it:
                    round_(it, False, False)
                round_(NG // U - 1, False, True)
                norm_routed(nm, ve, NG - 1)
                norm_settled(nm, ve)

            @block.scalar
            def _(ac):
                norm_begin_scalar(nm, ac)
                norm_root(nm, ac, 0, 0)

                def body(g, u, last, pair):
                    if not last:
                        norm_root(nm, ac, g + 1, (u + 1) % 2)
                    norm_turned(nm, ac, g, pair, u)

                with ac.Fori(0, NG // 2 - 1) as it:
                    for u in range(2):
                        body(it * 2 + u, u, False, it)
                for u in range(2):
                    body(NG - 2 + u, u, u == 1, NG // 2 - 1)

            @block.tensor
            def _(pe):
                norm_begin_tensor(nm, pe)
                pe.wait_ge(s_c, 2 * DMA)
                with pe.Fori(0, NG // 2) as it:
                    for u in range(2):
                        norm_turn(nm, pe, it * 2 + u, u)
                        norm_route(nm, pe, it * 2 + u, u)


def route_phase(nc, name, logits, weight, consts, We, we, s_we):
    before_in, order_in = consts
    with ExitStack() as ctx:
        def sb(n, shape, dt=F32):
            return ctx.enter_context(nc.sbuf_tensor(f"{name}_{n}", shape, dt))

        N = NT * E
        before32 = sb("before32", [P, P])
        before = sb("before", [P, P], BF16)
        ones = sb("ones", [P, P], BF16)
        ones32 = sb("ones32", [P, NT])
        order = sb("order", [P, E])
        t1, t2 = sb("t1", [P, NT, E]), sb("t2", [P, NT, E])
        sel = [sb(f"sel{k}", [P, NT, E]) for k in range(TOPK)]
        top = [sb(f"top{k}", [P, NT]) for k in range(TOPK)]
        rank = sb("rank", [P, NT])
        wk = [sb(f"wk{k}", [P, NT]) for k in range(TOPK)]
        gap, den = sb("gap", [P, NT]), sb("den", [P, NT])
        chosen = sb("chosen", [P, NT, E], BF16)
        count = sb("count", [P, NT, E])
        upto = sb("upto", [P, NT, E])
        p_in = ctx.enter_context(nc.psum_tensor(f"{name}_p_in", [P, N], F32))
        p_all = ctx.enter_context(nc.psum_tensor(f"{name}_p_all", [P, N], F32))
        s_c, s_ch, s_g, s_e, s_ma, s_mm = (nc.alloc_semaphore(f"{name}_{n}")
                                           for n in ("const", "chain", "gap", "exp", "mask", "sums"))
        L = logits[:, :].rearrange("p (t e) -> p t e", e=E)

        def over_e(ap):
            return ap.unsqueeze(2).to_broadcast([P, NT, E])

        with nc.Block() as block:
            @block.sync
            def _(sp):
                sp.dma_start(before32[:, :], before_in).then_inc(s_c, DMA)
                sp.dma_start(order[:, :], order_in).then_inc(s_c, DMA)
                sp.dma_start(we[:, :, :, :], We).then_inc(s_we, DMA)

            @block.vector
            def _(ve):
                ch = Chain(ve, s_ch, None, None)
                ve.memset(ones32[:, :], 1.0)
                ch.step(ve.memset(ones[:, :], 1.0))
                ve.wait_ge(s_c, 2 * DMA)
                ch.step(ve.tensor_copy(before[:, :], before32[:, :]))
                left = L
                for k in range(TOPK):
                    ch.step(ve.tensor_reduce(out=top[k][:, :], in_=left, op=ALU.max, axis=AX.X))
                    ch.step(ve.tensor_tensor(t1[:, :, :], left, over_e(top[k][:, :]), ALU.is_ge))
                    ch.step(ve.tensor_tensor(t2[:, :, :], t1[:, :, :],
                                             order[:, :].unsqueeze(1).to_broadcast([P, NT, E]), ALU.mult))
                    ch.step(ve.tensor_reduce(out=rank[:, :], in_=t2[:, :, :], op=ALU.max, axis=AX.X))
                    ch.step(ve.tensor_tensor(sel[k][:, :, :], t2[:, :, :], over_e(rank[:, :]), ALU.is_equal))
                    if k == 0:
                        ch.step(ve.scalar_tensor_tensor(out=upto[:, :, :], in0=sel[0][:, :, :], scalar=-3e38,
                                                        in1=L, op0=ALU.mult, op1=ALU.add))
                        left = upto[:, :, :]
                ch.step(ve.tensor_tensor(chosen[:, :, :], sel[0][:, :, :], sel[1][:, :, :], ALU.add))
                ve.sem_inc(s_ma, 1)
                ve.tensor_tensor(gap[:, :], top[1][:, :], top[0][:, :], ALU.subtract).then_inc(s_g, 1)
                ve.wait_ge(s_e, 1)
                ch.step(ve.tensor_scalar(den[:, :], wk[1][:, :], 1.0, None, ALU.add))
                ch.step(ve.reciprocal(wk[0][:, :], den[:, :]))
                ch.step(ve.tensor_tensor(gap[:, :], wk[1][:, :], wk[0][:, :], ALU.mult))
                ch.step(ve.tensor_tensor(t1[:, :, :], sel[0][:, :, :], over_e(wk[0][:, :]), ALU.mult))
                ch.step(ve.tensor_tensor(t2[:, :, :], sel[1][:, :, :], over_e(gap[:, :]), ALU.mult))
                ch.step(ve.tensor_tensor(sel[0][:, :, :], t1[:, :, :], t2[:, :, :], ALU.add))
                ve.wait_ge(s_mm, 1)
                ch.step(ve.tensor_copy(count[:, :, :].rearrange("p t e -> p (t e)"), p_all[:, :]))
                for b in range(B):
                    for e in range(E):
                        ts = slice(b * NT // B, (b + 1) * NT // B)
                        ve_last = ve.tensor_tensor_scan(out=upto[:, ts, e], data0=ones32[:, ts],
                                                        data1=count[:, ts, e], initial=0.0,
                                                        op0=ALU.mult, op1=ALU.add)
                ch.step(ve_last)
                ch.step(ve.tensor_tensor(t1[:, :, :], upto[:, :, :], count[:, :, :], ALU.subtract))
                ch.step(ve.tensor_tensor(t2[:, :, :].rearrange("p t e -> p (t e)"),
                                         t1[:, :, :].rearrange("p t e -> p (t e)"), p_in[:, :], ALU.add))
                ch.step(ve.tensor_scalar(t1[:, :, :], t2[:, :, :], float(CAP), 0.5, ALU.is_lt, ALU.mult))
                ch.step(ve.tensor_tensor(weight[:, :, :], t1[:, :, :], sel[0][:, :, :], ALU.mult))

            @block.scalar
            def _(ac):
                ac.wait_ge(s_g, 1)
                ac.activation(wk[1][:, :], gap[:, :], ACT.Exp).then_inc(s_e, 1)

            @block.tensor
            def _(pe):
                pe.wait_ge(s_ma, 1)
                ch_flat = chosen[:, :, :].rearrange("p t e -> p (t e)")
                pe.matmul(p_in[:, :], before[:, :], ch_flat, start=True, stop=True)
                pe.matmul(p_all[:, :], ones[:, :], ch_flat, start=True, stop=True).then_inc(s_mm, 1)


def expert_phase(nc, name, x, xnT, we, s_we, weight, out, then=None):
    EP = 2
    NP = E // EP
    PAIRS = TG * NP
    STEPS = TG * E
    with ExitStack() as ctx:
        def sb(n, shape, dt=F32):
            return ctx.enter_context(nc.sbuf_tensor(f"{name}_{n}", shape, dt))

        def sem(n):
            return nc.alloc_semaphore(f"{name}_{n}")

        xt = [sb(f"xt{u}", [P, NC, GT]) for u in range(2)]
        xg = [sb(f"x{u}", [P, TG, D]) for u in range(2)]
        acc = [sb(f"acc{u}", [P, TG, D]) for u in range(2)]
        acb = [sb(f"acb{u}", [P, TG, D]) for u in range(2)]
        ps = [ctx.enter_context(nc.psum_tensor(f"{name}_ps{k}", [P, EP * D], F32)) for k in range(NP)]
        s_id = sem("ident")
        s_xt = [sem(f"xt{u}") for u in range(2)]
        s_x = [sem(f"x{u}") for u in range(2)]
        s_st = [sem(f"st{u}") for u in range(2)]
        s_mm = sem("mm")
        s_ac = sem("acc")
        s_tick = sem("tick")
        nm = None
        if then is not None:
            ident = sb("ident", [P, P])
            nm = norm_buffers(nc, ctx, name + "_n", ident, then[1])

        def groups(eng, body, after):
            for u in range(2):
                body(u, u, 0, u == 0)
            with eng.Fori(1, NG // 2) as it:
                for u in range(2):
                    body(it * 2 + u, u, it, False)
            after()

        with nc.Block() as block:
            @block.sync
            def _(sp):
                def load(g, u):
                    hold(sp, s_ac, g * STEPS + STEPS, s_tick)
                    sp.dma_start(xt[u][:, :, :], xnT[bass.ds(g, 1), :, :, :].rearrange("g p c t -> p (g c) t"))\
                      .then_inc(s_xt[u], DMA)
                    sp.dma_start(xg[u][:, :, :], x[bass.ds(g, 1), :, :, :].rearrange("g p i d -> p (g i) d"))\
                      .then_inc(s_x[u], DMA)

                def store(g, u):
                    hold(sp, s_ac, g * STEPS + 3 * STEPS, s_tick)
                    sp.dma_start(out[bass.ds(g, 1), :, :, :].rearrange("g p i d -> p (g i) d"),
                                 acc[u][:, :, :]).then_inc(s_st[u], DMA)

                for u in range(2):
                    load(u, u)
                if nm:
                    sp.dma_start(ident[:, :], then[0]).then_inc(s_id, DMA)
                with sp.Fori(0, NG // 2 - 1) as it:
                    for u in range(2):
                        store(it * 2 + u, u)
                        load(it * 2 + (u + 2), u)
                        if nm:
                            norm_store(nm, sp, it * 2 + u, u)
                for u in range(2):
                    store(NG - 2 + u, u)
                    if nm:
                        norm_store(nm, sp, NG - 2 + u, u)
                for u in range(2):
                    sp.wait_ge(s_st[u], DMA * (NG // 2 + 1))
                if nm:
                    norm_stored(nm, sp)

            @block.tensor
            def _(pe):
                pe.wait_ge(s_we, DMA)
                if nm:
                    norm_begin_tensor(nm, pe)

                def body(g, u, it, first):
                    pe.wait_ge(s_xt[u], it * DMA + DMA)
                    for i in range(TG):
                        for k in range(NP):
                            pe.wait_ge(s_ac, g * STEPS + (2 * STEPS + (i - 1) * E + (k + 1) * EP))
                            for c in range(NC):
                                last = pe.matmul(ps[k][:, :], xt[u][:, c, i * P:(i + 1) * P],
                                                 we[:, c, EP * k:EP * k + EP, :].rearrange("p e f -> p (e f)"),
                                                 start=(c == 0), stop=(c == NC - 1))
                            last.then_inc(s_mm, 1)
                        if nm and i == TG // 2 and not first:
                            norm_turn(nm, pe, g - 1, 1 - u)
                    if nm and first:
                        pe.wait_ge(s_id, DMA)

                groups(pe, body, lambda: nm and norm_turn(nm, pe, NG - 1, 1))

            @block.vector
            def _(ve):
                ve.sem_inc(s_ac, 2 * STEPS)
                for u in range(2):
                    ve.sem_inc(s_st[u], DMA)
                if nm:
                    norm_begin_vector(nm, ve)

                def body(g, u, it, first):
                    ve.wait_ge(s_x[u], it * DMA + DMA)
                    ve.wait_ge(s_st[u], it * DMA + DMA)
                    if nm:
                        ve.wait_ge(nm.s_xn, g + 1)
                    for i in range(TG):
                        for e in range(E):
                            n = i * E + e
                            if e % EP == 0:
                                ve.wait_ge(s_mm, g * PAIRS + (i * NP + e // EP + 1))
                            if e:
                                ve.wait_ge(s_ac, g * STEPS + (2 * STEPS + n))
                            src = xg if e == 0 else (acb, acc)[(e - 1) % 2]
                            dst = (acb, acc)[e % 2]
                            ve.scalar_tensor_tensor(
                                out=dst[u][:, i, :], in0=ps[e // EP][:, (e % EP) * D:(e % EP + 1) * D],
                                scalar=weight[:, bass.ds(g * TG + i, 1), e],
                                in1=src[u][:, i, :], op0=ALU.mult, op1=ALU.add).then_inc(s_ac, 1)
                        if nm and i == 0 and not first:
                            normalise(nm, ve, g - 1, 1 - u, acc[1 - u])
                    if nm:
                        hold(ve, s_ac, g * STEPS + 3 * STEPS, s_tick)
                        norm_statistics(nm, ve, g, u, acc[u])

                groups(ve, body, lambda: nm and normalise(nm, ve, NG - 1, 1, acc[1]))

            if nm:
                @block.scalar
                def _(ac):
                    norm_begin_scalar(nm, ac)

                    def body(g, u, it, first):
                        if not first:
                            norm_turned(nm, ac, g - 1, it - (1 - u), 1 - u)
                        norm_root(nm, ac, g, u)

                    groups(ac, body, lambda: norm_turned(nm, ac, NG - 1, NG // 2 - 1, 1))


def qkv_phase(nc, name, xnT, wts, biases, tables, parts, v_out):
    wqk_in, wv_in = wts
    bqk_in, bv_in = biases
    cos_in, sin_in = tables
    R = 4
    N_PARTS = 3
    with ExitStack() as ctx:
        def sb(n, shape, dt=F32):
            return ctx.enter_context(nc.sbuf_tensor(f"{name}_{n}", shape, dt))

        def sem(n):
            return nc.alloc_semaphore(f"{name}_{n}")

        wqk, wv = sb("wqk", [P, NC, 4, P]), sb("wv", [P, NC, D])
        bqk, bv, bs = sb("bqk", [P, 4]), sb("bv", [P, D]), sb("bs", [P, 4])
        xt = [sb(f"xt{r}", [P, NC, GT]) for r in range(R)]
        cs = [sb(f"cs{r}", [P, 2, GT]) for r in range(R)]
        ev, od = sb("even", [P, 2, GT]), sb("odd", [P, 2, GT])
        ec, es, oc, os_ = (sb(n, [P, 2, GT]) for n in ("ec", "es", "oc", "os"))
        rot = sb("rot", [P, 2, 2, GT])
        rest = sb("rest", [P, 2, 2, GT])
        pt = [[sb(f"part{n}{u}", [P, 2, 2, GT], BF16) for n in range(N_PARTS)] for u in range(2)]
        vt = [sb(f"v{u}", [P, H, TG, HD]) for u in range(2)]
        pqk = [ctx.enter_context(nc.psum_tensor(f"{name}_pqk{k}", [P, GT], F32)) for k in range(4)]
        pv = [ctx.enter_context(nc.psum_tensor(f"{name}_pv{k}", [P, 2 * D], F32)) for k in range(4)]

        s_c = sem("const")
        s_bs = sem("bs")
        s_xt = [sem(f"xt{r}") for r in range(R)]
        s_cs = [sem(f"cs{r}") for r in range(R)]
        s_st = [sem(f"st{u}") for u in range(2)]
        s_sv = [sem(f"sv{u}") for u in range(2)]
        s_qk = sem("qk")
        s_v = sem("v")
        s_ev = sem("evac")
        s_vc = sem("vcopy")
        s_mu = sem("mult")
        s_po = sem("pool")
        s_r = sem("rot")
        s_hi = sem("hi")
        s_r1 = sem("rest")
        s_mi = sem("mid")
        s_lo = sem("lo")
        s_tick = sem("tick")

        def rounds(eng, body):
            with eng.Fori(0, NG // R - 1) as it:
                for r in range(R):
                    body(it * R + r, r, it, False)
            for r in range(R):
                body(NG - R + r, r, NG // R - 1, r == R - 1)

        def table(r):
            return [cs[r][:, k:k + 1, :].to_broadcast([P, 2, GT]) for k in range(2)]

        with nc.Block() as block:
            @block.sync
            def _(sp):
                for dst, src in ((wqk[:, :, :, :], wqk_in), (wv[:, :, :], wv_in), (bqk[:, :], bqk_in),
                                 (bv[:, :], bv_in)):
                    sp.dma_start(dst, src).then_inc(s_c, DMA)

                def load(g, r):
                    sp.dma_start(xt[r][:, :, :], xnT[bass.ds(g, 1), :, :, :].rearrange("g p c t -> p (g c) t"))\
                      .then_inc(s_xt[r], DMA)
                    for k, tab in enumerate((cos_in, sin_in)):
                        sp.dma_start(cs[r][:, k:k + 1, :], tab[:, bass.ds(g, 1), :]).then_inc(s_cs[r], DMA)

                for r in range(R):
                    load(r, r)

                def body(g, r, it, last):
                    u = r % 2
                    hold(sp, s_vc, g + 3, s_tick)
                    sp.dma_start(v_out[:, :, bass.ds(g, 1), :].rearrange("p h g n -> p h (g n)"),
                                 vt[u][:, :, :, :].rearrange("p h i d -> p h (i d)")).then_inc(s_sv[u], DMA)
                    hold(sp, s_lo, g + 2, s_tick)
                    for n in range(N_PARTS):
                        for half in range(2):
                            for w in range(2):
                                sp.dma_start(
                                    parts[w][n, half, :, bass.ds(g, 1), :].rearrange("p g t -> p (g t)"),
                                    pt[u][n][:, half, w, :]).then_inc(s_st[u], DMA)
                    if not isinstance(g, int):
                        load(g + R, r)

                rounds(sp, body)
                for u in range(2):
                    sp.wait_ge(s_st[u], DMA * (4 * N_PARTS * NG // 2 + 1))
                    sp.wait_ge(s_sv[u], DMA * (NG // 2 + 1))

            @block.tensor
            def _(pe):
                pe.wait_ge(s_c, 4 * DMA)

                def body(g, r, it, last):
                    pe.wait_ge(s_xt[r], it * DMA + DMA)
                    pe.wait_ge(s_ev, g + 1)
                    for m in range(4):
                        for c in range(NC):
                            mm = pe.matmul(pqk[m][:, :], wqk[:, c, m, :], xt[r][:, c, :],
                                           start=(c == 0), stop=(c == NC - 1))
                    mm.then_inc(s_qk, 1)
                    pe.wait_ge(s_vc, g + 1)
                    for i in range(TG):
                        for c in range(NC):
                            mm = pe.matmul(pv[2 * (r % 2) + i // 2][:, (i % 2) * D:(i % 2 + 1) * D],
                                           xt[r][:, c, i * P:(i + 1) * P], wv[:, c, :],
                                           start=(c == 0), stop=(c == NC - 1))
                    mm.then_inc(s_v, 1)

                rounds(pe, body)

            @block.scalar
            def _(ac):
                ac.sem_inc(s_ev, 1)
                ac.wait_ge(s_c, 4 * DMA)
                ac.activation(bs[:, 0:2], bqk[:, 0:2], ACT.Copy, scale=SCALE)
                ac.activation(bs[:, 2:4], bqk[:, 2:4], ACT.Copy).then_inc(s_bs, 1)
                ac.wait_ge(s_bs, 1)

                def evacuate(g):
                    ac.wait_ge(s_qk, g + 1)
                    ac.wait_ge(s_r, g + 1)
                    for m in range(4):
                        dst = (ev, od)[m % 2]
                        act = ac.activation(dst[:, m // 2, :], pqk[m][:, :], ACT.Identity,
                                            bias=bs[:, m:m + 1], scale=SCALE if m < 2 else 1.0)
                    act.then_inc(s_ev, 1)

                evacuate(0)

                def body(g, r, it, last):
                    u = r % 2
                    ac.wait_ge(s_st[u], it * (4 * N_PARTS * DMA * R // 2) + (4 * N_PARTS * DMA * (r // 2) + DMA))
                    ac.wait_ge(s_r, g + 2)
                    ac.activation(pt[u][0][:, :, :, :], rot[:, :, :, :], ACT.Copy).then_inc(s_hi, 1)
                    if not last:
                        evacuate(g + 1)
                    ac.wait_ge(s_r1, g + 2)
                    ac.activation(pt[u][1][:, :, :, :], rest[:, :, :, :], ACT.Copy).then_inc(s_mi, 1)

                rounds(ac, body)

            @block.vector
            def _(ve):
                for s in (s_r, s_r1, s_lo):
                    ve.sem_inc(s, 1)
                ve.sem_inc(s_vc, 2)
                for u in range(2):
                    ve.sem_inc(s_st[u], DMA)
                    ve.sem_inc(s_sv[u], DMA)
                ve.wait_ge(s_c, 4 * DMA)

                def products(g, r, it):
                    cos, sin = table(r)
                    ve.wait_ge(s_cs[r], it * (2 * DMA) + 2 * DMA)
                    ve.wait_ge(s_ev, g + 2)
                    ve.wait_ge(s_r, g + 1)
                    ve.tensor_tensor(ec[:, :, :], ev[:, :, :], cos, ALU.mult)
                    ve.tensor_tensor(os_[:, :, :], od[:, :, :], sin, ALU.mult).then_inc(s_mu, 1)

                def rotate(g):
                    ve.wait_ge(s_mu, g + 1)
                    ve.wait_ge(s_r1, g + 1)
                    ve.tensor_tensor(rot[:, 0, :, :], ec[:, :, :], os_[:, :, :], ALU.subtract)
                    ve.wait_ge(s_po, g + 1)
                    ve.tensor_tensor(rot[:, 1, :, :], es[:, :, :], oc[:, :, :], ALU.add).then_inc(s_r, 1)

                def values(g, r, it):
                    u = r % 2
                    ve.wait_ge(s_v, g + 1)
                    ve.wait_ge(s_sv[u], it * (DMA * R // 2) + (DMA * (r // 2) + DMA))
                    for i in range(TG):
                        add = ve.tensor_tensor(
                            vt[u][:, :, i, :],
                            pv[2 * u + i // 2][:, (i % 2) * D:(i % 2 + 1) * D].rearrange("p (h d) -> p h d", d=HD),
                            bv[:, :].rearrange("p (h d) -> p h d", d=HD), ALU.add)
                    add.then_inc(s_vc, 1)

                products(0, 0, 0)
                rotate(0)
                values(0, 0, 0)

                def body(g, r, it, last):
                    u, after = r % 2, (g + 1, (r + 1) % R, it + (r + 1) // R)
                    ve.wait_ge(s_hi, g + 1)
                    ve.wait_ge(s_lo, g + 1)
                    ve.tensor_tensor(rest[:, :, :, :], rot[:, :, :, :], pt[u][0][:, :, :, :],
                                     ALU.subtract).then_inc(s_r1, 1)
                    if not last:
                        products(*after)
                    ve.wait_ge(s_mi, g + 1)
                    ve.tensor_tensor(pt[u][2][:, :, :, :], rest[:, :, :, :], pt[u][1][:, :, :, :],
                                     ALU.subtract).then_inc(s_lo, 1)
                    if not last:
                        rotate(g + 1)
                        values(*after)

                rounds(ve, body)

            @block.gpsimd
            def _(gp):
                def body(g, r, it, last):
                    cos, sin = table(r)
                    gp.wait_ge(s_cs[r], it * (2 * DMA) + 2 * DMA)
                    gp.wait_ge(s_ev, g + 2)
                    gp.wait_ge(s_r, g + 1)
                    gp.tensor_tensor(es[:, :, :], ev[:, :, :], sin, ALU.mult)
                    gp.tensor_tensor(oc[:, :, :], od[:, :, :], cos, ALU.mult).then_inc(s_po, 1)

                rounds(gp, body)


def attend_phase(nc, name, parts, v_in, out, rows_dram):
    q_parts, k_parts = parts
    NH = B * H
    QB = 512
    QUAD = 4
    QU = QUAD * QB
    SB = S // QU
    KT = S // P
    TQ = QU // P
    KC = 2
    TERMS = [(0, 0), (0, 1), (0, 2), (1, 0), (1, 1), (2, 0)]
    ROWS = HD * len(TERMS)
    NB = 2
    NS = 3
    NX = 4
    TILES = KT * QUAD
    COPY_AT = QUAD
    SLOTS = TILES + 1
    AHEAD = TILES // 4
    PAIRS = TQ * S // (QB * KC)
    W = 32
    CH = 6
    BL = 32
    assert SLOTS % NS == 0 and KT % NX == 0 and PAIRS * KC == TILES and SB == 2
    assert AHEAD % (S // QB) == 0 and AHEAD // KC > CH
    with ExitStack() as ctx:
        def sb(n, shape, dt=F32):
            return ctx.enter_context(nc.sbuf_tensor(f"{name}_{n}", shape, dt))

        def sem(n):
            return nc.alloc_semaphore(f"{name}_{n}")

        Q = [sb(f"q{p}", [P, S], BF16) for p in range(NB)]
        K = [sb(f"k{p}", [P, S], BF16) for p in range(NB)]
        vst = [sb(f"vst{p}", [P, KT, HD]) for p in range(NB)]
        V = [sb(f"v{p}", [P, KT, W]) for p in range(NB)]
        Vl = sb("vlast", [P, W])
        Ex = [sb(f"ex{j}", [P, QB]) for j in range(NX * QUAD)]
        O = sb("o", [P, QB])
        mx = sb("mx", [P, TQ, PAIRS // TQ])
        nm, rest, rest2 = sb("nm", [P, TQ]), sb("rest", [P, TQ]), sb("rest2", [P, TQ])
        m3 = sb("m3", [P, 2 * BL], BF16)
        m3T = sb("m3T", [P, 2 * BL], BF16)
        ps = [ctx.enter_context(nc.psum_tensor(f"{name}_s{k}", [P, QB], F32)) for k in range(NS)]
        pm = [ctx.enter_context(nc.psum_tensor(f"{name}_m{k}", [P, KC * QB], F32)) for k in range(2)]
        po = ctx.enter_context(nc.psum_tensor(f"{name}_po", [P, QB], F32))

        s_ld = [sem(f"load{p}") for p in range(NB)]
        s_lv = [sem(f"loadv{p}") for p in range(NB)]
        s_vh = sem("vh")
        s_vl = sem("vl")
        s_one = sem("ones")
        s_s = sem("scores")
        s_e = sem("exp")
        s_pv = sem("pv")
        s_m = sem("mtile")
        s_mr = sem("mred")
        s_ch = sem("chain")
        s_m3 = sem("m3")
        s_row = sem("rowout")
        s_mq = sem("mq")
        s_out = sem("out")
        s_tick = sem("tick")
        LOADS = 2 * len(TERMS)

        def slot(j):
            return j if j < COPY_AT else j + 1

        def load(sp, p, h):
            for t, (a, b) in enumerate(TERMS):
                rows = slice(HD * t, HD * (t + 1))
                for dst, src in ((Q[p][rows, :], q_parts[a]), (K[p][rows, :], k_parts[b])):
                    sp.dma_start(dst, src[:, bass.ds(h, 1), :].rearrange("r h s -> r (h s)"))\
                      .then_inc(s_ld[p], DMA)
            sp.dma_start(vst[p][:, :, :],
                         v_in[:, bass.ds(h, 1), :].rearrange("p h n -> p (h n)").rearrange("p (k d) -> p k d", d=HD))\
              .then_inc(s_lv[p], DMA)

        def heads(eng, step):
            full = (NH - 2) // NB
            assert full * NB == NH - 2
            with eng.Fori(0, full) as n:
                for r in range(NB):
                    step(r, n * NB + r, n, True)
            step(0, NH - 2, full, True)
            step(1, NH - 1, full, False)

        with nc.Block() as block:
            @block.sync
            def _(sp):
                load(sp, 0, 0)

                def rows_of_max(p, sb_, w):
                    hold(sp, s_m3, w + 3, s_tick)
                    sp.dma_start(rows_dram[bass.ds(w, 1), :, :].rearrange("w p r -> p (w r)"), m3T[:, :])\
                      .then_inc(s_row, DMA)
                    hold(sp, s_row, w * DMA + 3 * DMA, s_tick)
                    src = rows_dram[bass.ds(w, 1), :, :].rearrange("w (b c) r -> b (w c) r", b=P // BL)
                    for k in range(3):
                        c, half = TQ * k % BL, TQ * k // BL
                        sp.dma_start(
                            Q[p][ROWS + k:ROWS + k + 1, bass.ds(sb_ * QU, QU)]
                            .rearrange("p (i b r) -> p i b r", b=P // BL, r=BL),
                            src[:, c:c + TQ, half * BL:(half + 1) * BL].rearrange("b i r -> i b r").unsqueeze(0))\
                          .then_inc(s_mq, DMA)
                    hold(sp, s_mq, w * (3 * DMA) + 3 * DMA, s_tick)

                rows_of_max(0, 0, 0)

                def step(r, h, n, more):
                    if more:
                        hold(sp, s_pv, h * (SB * KT) + (NX - 1 + 1), s_tick)
                        hold(sp, s_vh, h + 1, s_tick)
                        load(sp, 1 - r, h + 1)
                    for sb_ in range(SB):
                        u = h * SB + sb_
                        if sb_ < SB - 1:
                            rows_of_max(r, sb_ + 1, u + 1)
                        elif more:
                            rows_of_max(1 - r, 0, u + 1)
                        hold(sp, s_e, u * SLOTS + (SLOTS + COPY_AT + 1 + NS), s_tick)
                        for g in range(QUAD):
                            sp.dma_start(out[:, bass.ds(h, 1), bass.ds(sb_ * QU + g * QB, QB)]
                                         .rearrange("d h s -> d (h s)"),
                                         O[W * g:W * g + HD + 1, :]).then_inc(s_out, DMA)

                heads(sp, step)
                sp.wait_ge(s_out, (NH * SB + 2) * QUAD * DMA)

            @block.gpsimd
            def _(gp):
                for p in range(NB):
                    gp.memset(V[p][:, :, :], 0.0)
                gp.memset(Vl[:, :], 1.0)
                for j in range(QUAD):
                    last = gp.memset(Ex[(NX - 1) * QUAD + j][:, :], 1.0)
                last.then_inc(s_one, 1)
                gp.wait_ge(s_one, 1)
                for p in range(NB):
                    last = gp.memset(V[p][:, :, HD:HD + 1], 1.0)
                last.then_inc(s_one, 1)
                gp.wait_ge(s_one, 2)
                for p in range(NB):
                    last = gp.memset(K[p][ROWS:ROWS + 3, :], 1.0)
                last.then_inc(s_one, 1)
                gp.wait_ge(s_one, 3)

                def fill(p, n):
                    hold(gp, s_lv[p], n * DMA + DMA, s_tick)
                    gp.tensor_copy(V[p][:, :, 0:HD], vst[p][:, :, :]).then_inc(s_vh, 1)

                fill(0, 0)

                def step(r, h, n, more):
                    hold(gp, s_pv, h * (SB * KT) + (NX - 1 + 1), s_tick)
                    hold(gp, s_vh, h + 1, s_tick)
                    gp.tensor_copy(Vl[:, :], V[r][:, KT - 1, :]).then_inc(s_vl, 1)
                    if more:
                        fill(1 - r, n + r)

                heads(gp, step)

            @block.tensor
            def _(pe):
                pe.sem_inc(s_pv, NX - 1)
                pe.sem_inc(s_vl, 1)
                pe.wait_ge(s_one, 2)

                def max_chunk(k, p, column, w):
                    c = k % (S // QB)
                    if c % KC == 0:
                        pe.wait_ge(s_mr, w * PAIRS + (k // KC + 1))
                    ins = pe.matmul(pm[(k // KC) % 2][:, (c % KC) * QB:(c % KC + 1) * QB],
                                    Q[p][0:ROWS, bass.ds(column, P)],
                                    K[p][0:ROWS, c * QB:(c + 1) * QB], start=True, stop=True)
                    if c % KC == KC - 1:
                        ins.then_inc(s_m, 1)

                def find(k, r, sb_, u, more, loaded):
                    ahead = sb_ + 1 + (k + AHEAD) // TILES
                    k = (k + AHEAD) % TILES
                    if ahead >= SB and not more:
                        return
                    if ahead == SB and k == 0:
                        hold(pe, *loaded, s_tick)
                    max_chunk(k, r if ahead < SB else 1 - r,
                              ahead % SB * QU + k // (S // QB) * P, u + (ahead - sb_))

                def times_v(v, j, start=None, stop=None):
                    for g in range(QUAD):
                        last = pe.matmul(po[W * g:W * (g + 1), :], v, Ex[QUAD * (j % NX) + g][:, :],
                                         start=(j == 0) if start is None else start,
                                         stop=(j == KT - 1) if stop is None else stop)
                    return last

                def last_quad(u, set_apart):
                    pe.wait_ge(s_vl, set_apart)
                    pe.wait_ge(s_e, u * SLOTS + NS)
                    times_v(Vl[:, :], KT - 1).then_inc(s_pv, 1)

                def unit(p, sb_, u, h, more, loaded):
                    pe.wait_ge(s_mq, u * (3 * DMA) + 3 * DMA)
                    for j in range(KT):
                        for g in range(QUAD):
                            k = j * QUAD + g
                            pe.wait_ge(s_e, u * SLOTS + (slot(k) + 1))
                            pe.matmul(ps[slot(k) % NS][:, :], K[p][0:ROWS + 3, j * P:(j + 1) * P],
                                      Q[p][0:ROWS + 3, sb_ * QU + g * QB:sb_ * QU + (g + 1) * QB],
                                      start=True, stop=True).then_inc(s_s, 1)
                            find(k, p, sb_, u, more, loaded)
                        if j == 0:
                            last_quad(u, h + sb_ + 1)
                        else:
                            pe.wait_ge(s_e, u * SLOTS + (max(slot(QUAD * j - 1), COPY_AT) + 1 + NS))
                            times_v(V[p][:, j - 1, :], j - 1).then_inc(s_pv, 1)

                times_v(Vl[:, :], NX - 1, True, False)
                pe.wait_ge(s_ld[0], LOADS * DMA)
                with pe.Fori(0, (TILES + AHEAD) // (S // QB)) as i:
                    for c in range(S // QB):
                        if c % KC == 0:
                            pe.wait_ge(s_mr, i * (S // QB // KC) + (c // KC + 1))
                        ins = pe.matmul(pm[(c // KC) % 2][:, (c % KC) * QB:(c % KC + 1) * QB],
                                        Q[0][0:ROWS, bass.ds(i * P, P)],
                                        K[0][0:ROWS, c * QB:(c + 1) * QB], start=True, stop=True)
                        if c % KC == KC - 1:
                            ins.then_inc(s_m, 1)
                pe.wait_ge(s_one, 3)

                def step(r, h, n, more):
                    hold(pe, s_vh, h + 1, s_tick)
                    loaded = s_ld[1 - r], (n + r) * (LOADS * DMA) + LOADS * DMA
                    for sb_ in range(SB):
                        unit(r, sb_, h * SB + sb_, h, more, loaded)

                heads(pe, step)
                last_quad(NH * SB, NH + 1)

            @block.scalar
            def _(ac):
                ac.sem_inc(s_e, NS)

                def take_output(u):
                    ac.wait_ge(s_pv, u * KT + (NX - 1 + 1))
                    ac.wait_ge(s_out, u * (QUAD * DMA) + QUAD * DMA)
                    ac.activation(O[:, :], po[:, :], ACT.Copy).then_inc(s_e, 1)

                def unit(u):
                    for k in range(TILES):
                        if k % QUAD == 0:
                            ac.wait_ge(s_pv, u * KT + (k // QUAD + 1))
                        ac.wait_ge(s_s, u * TILES + (k + 1))
                        ac.activation(Ex[k % (NX * QUAD)][:, :], ps[slot(k) % NS][:, :], ACT.Exp)\
                          .then_inc(s_e, 1)
                        if k == COPY_AT - 1:
                            take_output(u)

                def step(r, h, n, more):
                    with ac.Fori(0, SB) as sb_:
                        unit(h * SB + sb_)

                heads(ac, step)
                take_output(NH * SB)
                ac.wait_ge(s_e, NH * SB * SLOTS + (NS + 1))
                ac.sem_inc(s_e, COPY_AT)

            @block.vector
            def _(ve):
                ve.sem_inc(s_mr, 2)
                ve.sem_inc(s_out, 2 * QUAD * DMA)
                ve.sem_inc(s_row, 2 * DMA)
                ve.sem_inc(s_m3, 1)
                ve.memset(m3[:, :], 0.0)
                ve.memset(nm[:, :], 0.0).then_inc(s_ch, 1)

                def find_max(k, w):
                    if k == 0:
                        ve.wait_ge(s_ch, w * CH + 1)
                    ve.wait_ge(s_m, w * PAIRS + (k + 1))
                    per = PAIRS // TQ
                    ve.tensor_reduce(out=mx[:, k // per, k % per:k % per + 1], in_=pm[k % 2][:, :],
                                     op=ALU.max, axis=AX.X).then_inc(s_mr, 1)

                def split(n, w):
                    ve.wait_ge(s_ch, w * CH + (n + 1))
                    part = [m3[:, TQ * k:TQ * (k + 1)] for k in range(3)]
                    if n == 0:
                        ve.wait_ge(s_m3, w + 1)
                        ve.tensor_copy(part[0], nm[:, :]).then_inc(s_ch, 1)
                    if n == 1:
                        ve.tensor_tensor(rest[:, :], nm[:, :], part[0], ALU.subtract).then_inc(s_ch, 1)
                    if n == 2:
                        ve.tensor_copy(part[1], rest[:, :]).then_inc(s_ch, 1)
                    if n == 3:
                        ve.tensor_tensor(rest2[:, :], rest[:, :], part[1], ALU.subtract).then_inc(s_ch, 1)
                    if n == 4:
                        ve.tensor_copy(part[2], rest2[:, :]).then_inc(s_ch, 1)
                    if n == 5:
                        ve.wait_ge(s_row, w * DMA + DMA)
                        ve.transpose(m3T[:, :], m3[:, :]).then_inc(s_m3, 1)

                def unit(w):
                    for k in range(PAIRS):
                        find_max(k, w)
                        if k < CH:
                            split(k, w)
                    ve.wait_ge(s_mr, w * PAIRS + (PAIRS + 2))
                    ve.tensor_reduce(out=nm[:, :], in_=mx[:, :, :], op=ALU.max, axis=AX.X, negate=True)\
                      .then_inc(s_ch, 1)

                with ve.Fori(0, NH * SB) as w:
                    unit(w)
                for k in range(CH):
                    split(k, NH * SB)


def out_phase(nc, name, x, att, rec_dram, Wo, bo, consts, out, then):
    ident_in, spread_in = consts
    xnT, Wr, logits = then
    with ExitStack() as ctx:
        def sb(n, shape, dt=F32):
            return ctx.enter_context(nc.sbuf_tensor(f"{name}_{n}", shape, dt))

        def sem(n):
            return nc.alloc_semaphore(f"{name}_{n}")

        ident, wr = sb("ident", [P, P]), sb("wr", [P, NC, E])
        spread = sb("spread", [H, P])
        wo = sb("wo", [P, NC, D])
        bo_sb = sb("bo", [P, D])
        at = [sb(f"at{u}", [P, NC, GT]) for u in range(2)]
        alls = sb("sums", [P, H * B * S // P])
        allr = sb("recs", [P, H * B * S // P])
        rec = [sb(f"rec{u}", [H, GT]) for u in range(2)]
        an = [sb(f"an{u}", [P, NC, GT]) for u in range(2)]
        xg = [sb(f"x{u}", [P, TG, D]) for u in range(2)]
        xb = [sb(f"xb{u}", [P, TG, D]) for u in range(2)]
        y = [sb(f"y{u}", [P, TG, D]) for u in range(2)]
        pr = ctx.enter_context(nc.psum_tensor(f"{name}_pr", [P, GT], F32))
        py = [ctx.enter_context(nc.psum_tensor(f"{name}_py{k}", [P, 2 * D], F32)) for k in range(4)]
        s_c = sem("const")
        s_sum = sem("sums")
        s_all = sem("recs")
        s_rd = sem("recout")
        s_at = [sem(f"at{u}") for u in range(2)]
        s_rec = [sem(f"rec{u}") for u in range(2)]
        s_x = [sem(f"x{u}") for u in range(2)]
        s_st = [sem(f"st{u}") for u in range(2)]
        s_pr = sem("pr")
        s_an = sem("an")
        s_y = sem("y")
        s_xb = sem("xb")
        s_o = sem("out")
        s_tick = sem("tick")
        nm = norm_buffers(nc, ctx, name + "_n", ident, xnT, wr, logits)
        rows = att[0:HD, :, :, :].rearrange("d h b s -> (d h) b s").rearrange("(c p) b s -> p c b s", p=P)
        sums = att[HD:HD + 1, :, :, :].rearrange("o h b s -> (o h) b s")

        with nc.Block() as block:
            @block.sync
            def _(sp):
                sp.dma_start(alls[:, :], sums.rearrange("h b s -> (h b s)").rearrange("(p n) -> p n", p=P))\
                  .then_inc(s_sum, DMA)
                for dst, src in ((ident[:, :], ident_in), (wr[:, :, :], Wr), (spread[:, :], spread_in),
                                 (wo[:, :, :], Wo), (bo_sb[:, :], bo)):
                    sp.dma_start(dst, src).then_inc(s_c, DMA)


                def load(g, u):
                    tokens = bass.ds(g * GT, GT)
                    for c in range(NC):
                        sp.dma_start(at[u][:, c, :], rows[:, c, :, :].rearrange("p b s -> p (b s)")[:, tokens])\
                          .then_inc(s_at[u], DMA)
                    sp.dma_start(xg[u][:, :, :], x[bass.ds(g, 1), :, :, :].rearrange("g p i d -> p (g i) d"))\
                      .then_inc(s_x[u], DMA)

                def load_reciprocals(g, u):
                    sp.dma_start(rec[u][:, :], rec_dram.rearrange("h b s -> h (b s)")[:, bass.ds(g * GT, GT)])\
                      .then_inc(s_rec[u], DMA)

                def store(g, u):
                    sp.dma_start(out[bass.ds(g, 1), :, :, :].rearrange("g p i d -> p (g i) d"),
                                 y[u][:, :, :]).then_inc(s_st[u], DMA)

                for u in range(2):
                    load(u, u)
                sp.wait_ge(s_all, 1)
                sp.dma_start(rec_dram.rearrange("h b s -> (h b s)").rearrange("(p n) -> p n", p=P), allr[:, :])\
                  .then_inc(s_rd, DMA)
                sp.wait_ge(s_rd, DMA)
                for u in range(2):
                    load_reciprocals(u, u)
                with sp.Fori(0, NG // 2 - 1) as it:
                    for u in range(2):
                        g = it * 2 + u
                        hold(sp, s_o, g + 3, s_tick)
                        load_reciprocals(g + 2, u)
                        load(g + 2, u)
                        store(g, u)
                        norm_store(nm, sp, it * 2 + u, u)
                for u in range(2):
                    hold(sp, s_o, NG + 1 + u, s_tick)
                    store(NG - 2 + u, u)
                    norm_store(nm, sp, NG - 2 + u, u)
                for u in range(2):
                    sp.wait_ge(s_st[u], DMA * (NG // 2 + 1))
                norm_stored(nm, sp)

            def groups(eng, body):
                for u in range(2):
                    body(u, u, 0, u)
                with eng.Fori(1, NG // 2 - 1) as it:
                    for u in range(2):
                        body(it * 2 + u, u, it, 2)
                for u in range(2):
                    body(NG - 2 + u, u, NG // 2 - 1, NG - 2 + u)

            @block.scalar
            def _(ac):
                norm_begin_scalar(nm, ac)

                def body(g, u, it, nth):
                    if nth >= 1:
                        norm_turned(nm, ac, g - 1, it - (1 - u), 1 - u)
                    norm_root(nm, ac, g, u)

                groups(ac, body)
                norm_turned(nm, ac, NG - 1, NG // 2 - 1, 1)

            @block.tensor
            def _(pe):
                norm_begin_tensor(nm, pe)
                pe.wait_ge(s_c, 5 * DMA)

                def spread_out(g, u, times):
                    pe.wait_ge(s_rec[u], times * DMA + DMA)
                    pe.wait_ge(s_an, g + 1)
                    pe.matmul(pr[:, :], spread[:, :], rec[u][:, :], start=True, stop=True).then_inc(s_pr, 1)

                spread_out(0, 0, 0)

                def body(g, u, it, nth):
                    pe.wait_ge(s_an, g + 2)
                    pe.wait_ge(s_o, g + 1)
                    for i in range(TG):
                        for c in range(NC):
                            last = pe.matmul(py[2 * u + i // 2][:, (i % 2) * D:(i % 2 + 1) * D],
                                             an[u][:, c, i * P:(i + 1) * P], wo[:, c, :],
                                             start=(c == 0), stop=(c == NC - 1))
                    last.then_inc(s_y, 1)
                    if nth >= 2:
                        norm_route(nm, pe, g - 2, u)
                    if nth < NG - 1:
                        spread_out(g + 1, 1 - u, it + u)
                    if nth >= 1:
                        norm_turn(nm, pe, g - 1, 1 - u)

                groups(pe, body)
                norm_route(nm, pe, NG - 2, 0)
                norm_turn(nm, pe, NG - 1, 1)
                norm_route(nm, pe, NG - 1, 1)

            @block.gpsimd
            def _(gp):
                gp.wait_ge(s_c, 5 * DMA)
                with gp.Fori(0, NG // 2) as it:
                    for u in range(2):
                        gp.wait_ge(s_x[u], it * DMA + DMA)
                        gp.wait_ge(s_o, it * 2 + (u + 1))
                        for i in range(TG):
                            last = gp.tensor_tensor(xb[u][:, i, :], xg[u][:, i, :], bo_sb[:, :], ALU.add)
                        last.then_inc(s_xb, 1)

            @block.vector
            def _(ve):
                ve.sem_inc(s_an, 1)
                ve.sem_inc(s_o, 2)
                for u in range(2):
                    ve.sem_inc(s_st[u], DMA)
                norm_begin_vector(nm, ve)
                ve.wait_ge(s_sum, DMA)
                ve.reciprocal(allr[:, :], alls[:, :]).then_inc(s_all, 1)

                def normalise_heads(g, u, times):
                    ve.wait_ge(s_at[u], times * (2 * DMA) + 2 * DMA)
                    ve.wait_ge(s_pr, g + 1)
                    for c in range(NC):
                        last = ve.tensor_tensor(an[u][:, c, :], at[u][:, c, :], pr[:, :], ALU.mult)
                    last.then_inc(s_an, 1)

                normalise_heads(0, 0, 0)

                def body(g, u, it, nth):
                    if nth >= 1:
                        normalise(nm, ve, g - 1, 1 - u, y[1 - u])
                    ve.wait_ge(s_y, g + 1)
                    ve.wait_ge(s_xb, g + 1)
                    ve.wait_ge(s_st[u], it * DMA + DMA)
                    ve.wait_ge(nm.s_xn, g + 1)
                    for i in range(TG // 2):
                        last = ve.tensor_tensor(
                            y[u][:, 2 * i:2 * i + 2, :].rearrange("p i d -> p (i d)"), py[2 * u + i][:, :],
                            xb[u][:, 2 * i:2 * i + 2, :].rearrange("p i d -> p (i d)"), ALU.add)
                    last.then_inc(s_o, 1)
                    if nth < NG - 1:
                        normalise_heads(g + 1, 1 - u, it + u)
                    if nth >= 2:
                        norm_routed(nm, ve, g - 2)
                    hold(ve, s_o, g + 3, s_tick)
                    norm_statistics(nm, ve, g, u, y[u])

                groups(ve, body)
                norm_routed(nm, ve, NG - 2)
                normalise(nm, ve, NG - 1, 1, y[1])
                norm_routed(nm, ve, NG - 1)
                norm_settled(nm, ve)


def program(nc, x, w, c, out):
    def grouped(ap):
        return ap.rearrange("(g i p) d -> g p i d", i=TG, p=P)

    def dram(n, shape, dt=F32):
        return nc.dram_tensor(n, shape, dt, kind="Internal").ap()

    x1 = dram("after_ffn1", (NG, P, TG, D))
    x2 = dram("after_attention", (NG, P, TG, D))
    xnT = [dram(f"normalised{k}", (NG, P, NC, GT)) for k in range(3)]
    qk = [dram(f"{n}_parts", (3, 2, P, NG, GT), BF16) for n in "qk"]
    vd = dram("v_by_head", (P, H, NG, TG * HD))
    att = dram("attended", (HD + 1, H, B, S))
    recs = dram("reciprocals", (H, B, S))
    rows = dram("max_rows", (B * H * S // 2048, P, 64), BF16)

    with ExitStack() as ctx:
        logits = ctx.enter_context(nc.sbuf_tensor("logits", [P, NT * E], F32))
        weight = ctx.enter_context(nc.sbuf_tensor("weight", [P, NT, E], F32))

        def ffn(name, x, xnT, out, then=None):
            with nc.sbuf_tensor(f"{name}_we", [P, NC, E, D], F32) as we:
                s_we = nc.alloc_semaphore(f"{name}_we")
                route_phase(nc, name + "r", logits, weight, (c["before"], c["order"]), w["We"], we, s_we)
                expert_phase(nc, name + "e", x, xnT, we, s_we, weight, out, then)

        norm_phase(nc, "f1n", grouped(x), xnT[0], c["ident"], w["Wr"], logits)
        ffn("f1", grouped(x), xnT[0], x1, (c["ident"], xnT[1]))
        qkv_phase(nc, "ap", xnT[1], (w["Wqk"], w["Wv"]), (w["bqk"], w["bv"]), (c["cos"], c["sin"]), qk, vd)
        attend_phase(nc, "at",
                     [[t[k].rearrange("f (j h) (b g) t -> (f j) (h b) (g t)", h=H, b=B) for k in range(3)] for t in qk],
                     vd.rearrange("p h (b g) n -> p (h b) (g n)", b=B), att.rearrange("d h b s -> d (h b) s"), rows)
        out_phase(nc, "ao", x1, att, recs, w["Wo"], w["bo"], (c["ident"], c["spread"]), x2, (xnT[2], w["Wr"], logits))
        ffn("f2", x2, xnT[2], grouped(out))


def shape_constants():
    inv_freq = (np.float32(1.0) / np.float32(10000.0) ** (np.arange(0, HD, 2, dtype=np.float32) / np.float32(HD)))
    angle = np.arange(S, dtype=np.float32)[:, None] * inv_freq.astype(np.float32)[None, :]
    rows = np.repeat(np.arange(HD // 2), H)

    def table(f):
        t = f(angle).astype(np.float32)[:, rows].T.reshape(P, GB, GT)
        return np.ascontiguousarray(np.concatenate([t] * B, axis=1))

    return {
        "ident": np.eye(P, dtype=np.float32),
        "before": np.triu(np.ones((P, P), np.float32), 1),
        "order": np.tile(np.arange(E, 0, -1, dtype=np.float32), (P, 1)),
        "spread": np.tile(np.eye(H, dtype=np.float32), (1, P // H)),
        "cos": table(np.cos),
        "sin": table(np.sin),
    }


def kernel(L0_attn_x, L0_attn_Wq, L0_attn_bq, L0_attn_Wk, L0_attn_bk, L0_attn_Wv, L0_attn_bv,
           L0_attn_Wo, L0_attn_bo, L0_ffn_Wr, L0_ffn_We):
    import concourse.bacc as bacc
    from concourse.bass_utils import run_bass_kernel_spmd

    def by_feature(a):
        return a.T.reshape(NC, P, -1).transpose(1, 0, 2)

    def halves(W):
        return [W.reshape(H, HD // 2, 2, -1)[:, :, k, :].transpose(1, 0, 2).reshape(P, -1) for k in range(2)]

    X = {n: np.asarray(a) for n, a in dict(
        x=L0_attn_x, Wq=L0_attn_Wq, bq=L0_attn_bq, Wk=L0_attn_Wk, bk=L0_attn_bk, Wv=L0_attn_Wv,
        bv=L0_attn_bv, Wo=L0_attn_Wo, bo=L0_attn_bo, Wr=L0_ffn_Wr, We=L0_ffn_We).items()}
    arrays = {
        "x": X["x"].reshape(B * S, D),
        "Wqk": np.stack([by_feature(m) for m in halves(X["Wq"]) + halves(X["Wk"])], axis=2),
        "bqk": np.concatenate(halves(X["bq"].reshape(D, 1)) + halves(X["bk"].reshape(D, 1)), axis=1),
        "Wv": by_feature(X["Wv"]),
        "bv": np.tile(X["bv"], (P, 1)),
        "Wo": by_feature(X["Wo"].reshape(D, H, HD).transpose(0, 2, 1).reshape(D, D)),
        "bo": np.tile(X["bo"], (P, 1)),
        "Wr": by_feature(X["Wr"]),
        "We": X["We"].reshape(E, NC, P, D).transpose(2, 1, 0, 3),
    }
    consts = shape_constants()
    nc = bacc.Bacc("TRN2", target_bir_lowering=False, num_devices=1)
    given, aps = {}, {}
    for n, a in {**arrays, **{"c_" + k: v for k, v in consts.items()}}.items():
        given[f"in_{n}"] = np.ascontiguousarray(a)
        aps[n] = nc.dram_tensor(f"in_{n}", a.shape, F32, kind="ExternalInput").ap()
    out = nc.dram_tensor("out", (B * S, D), F32, kind="ExternalOutput").ap()
    program(nc, aps["x"], aps, {k: aps["c_" + k] for k in consts}, out)
    r = run_bass_kernel_spmd(nc, [given], core_ids=[0])
    return r.results[0]["out"].reshape(B, S, D)
```
